# Optimizing a Trainium2 kernel written in Bass

```python
import numpy as np
import jax
import jax.numpy as jnp

def _softmax(x, axis=-1):
    return jax.nn.softmax(x, axis=axis)

def _gelu(x):
    return jax.nn.gelu(x, approximate=True)

def _silu(x):
    return jax.nn.silu(x)

def _sigmoid(x):
    return jax.nn.sigmoid(x)

def _layernorm(x, axis=-1, eps=1e-05):
    m = jnp.mean(x, axis=axis, keepdims=True)
    v = jnp.var(x, axis=axis, keepdims=True)
    return (x - m) / jnp.sqrt(v + eps)

def _scatter_add(tgt, idx, src, axis=0):
    return tgt.at[idx].add(src)

def _segment_sum(src, seg, n):
    return jax.ops.segment_sum(src, seg, n)
kernel_name = 'mk_adj_preln_d2_adj_r2_030b0f'

def setup_inputs(seed: int=0):
    np.random.seed(seed)
    _w = jnp.asarray

    def _rec_inputs():
        import jax
        import jax.numpy as jnp
        _gk = jax.random.key(seed)
        x = -0.0005207 + 1.001 * jax.random.normal(jax.random.fold_in(_gk, 1), (4096, 128), jnp.float32)
        _a = jax.random.bernoulli(jax.random.fold_in(_gk, 2), 0.000488281, (4096, 4096))
        _a = jnp.logical_or(_a, jnp.swapaxes(_a, -1, -2))
        _a = jnp.logical_or(_a, jnp.eye(4096, dtype=bool))
        _af = _a.astype(jnp.float32)
        _af = _af * jax.random.uniform(jax.random.fold_in(_gk, 3), (4096, 4096), jnp.float32, 0.05, 1)
        adj = _af
        return (x, adj)
    x, adj = _rec_inputs()

    def _L0_gnn_setup():
        import jax, jax.numpy as jnp
        import numpy as np
        IN_DIM = 128
        OUT_DIM = 128
        N = 8192
        key = jax.random.key(seed)
        k_x, k_adj, k_w, k_b = jax.random.split(key, 4)
        x = jax.random.normal(k_x, (N, IN_DIM), dtype=jnp.float32)
        adj = jax.random.uniform(k_adj, (N, N), dtype=jnp.float32)
        bound = 1.0 / np.sqrt(2 * IN_DIM)
        W = jax.random.uniform(k_w, (OUT_DIM, 2 * IN_DIM), dtype=jnp.float32, minval=-bound, maxval=bound)
        b = jax.random.uniform(k_b, (OUT_DIM,), dtype=jnp.float32, minval=-bound, maxval=bound)
        return {'x': x, 'adj': adj, 'W': W, 'b': b}
    _L0_gnn_all = _L0_gnn_setup()
    _L0_gnn_in = {k: v for k, v in _L0_gnn_all.items() if k in ('W', 'b')}
    del _L0_gnn_all

    def _L1_gnn_setup():
        import jax, jax.numpy as jnp
        import numpy as np
        N, D_IN, D_HID, D_OUT, K = (5000, 128, 128, 128, 3)

        def cheb_conv(x, L, W, b):
            Tx0 = x
            out = Tx0 @ W[0]
            Tx1 = L @ x
            out = out + Tx1 @ W[1]
            for k in range(2, W.shape[0]):
                Tx2 = 2.0 * (L @ Tx1) - Tx0
                out = out + Tx2 @ W[k]
                Tx0, Tx1 = (Tx1, Tx2)
            return out + b
        key = jax.random.key(seed)
        ks = jax.random.split(key, 4)
        x = jax.random.normal(ks[0], (N, D_IN), dtype=jnp.float32)
        L = jax.random.normal(ks[1], (N, N), dtype=jnp.float32) / jnp.sqrt(jnp.float32(N))
        W0 = jax.random.normal(ks[2], (K, D_IN, D_HID), dtype=jnp.float32) / jnp.sqrt(jnp.float32(D_IN))
        b0 = jnp.zeros((D_HID,), dtype=jnp.float32)
        W1 = jax.random.normal(ks[3], (K, D_HID, D_OUT), dtype=jnp.float32) / jnp.sqrt(jnp.float32(D_HID))
        b1 = jnp.zeros((D_OUT,), dtype=jnp.float32)
        return {'x': x, 'L': L, 'W0': W0, 'b0': b0, 'W1': W1, 'b1': b1}
    _L1_gnn_all = _L1_gnn_setup()
    _L1_gnn_in = {k: v for k, v in _L1_gnn_all.items() if k in ('W0', 'b0', 'W1', 'b1')}
    del _L1_gnn_all
    return {'x': x, 'adj': adj, 'L0_gnn_W': _L0_gnn_in['W'], 'L0_gnn_b': _L0_gnn_in['b'], 'L1_gnn_W0': _L1_gnn_in['W0'], 'L1_gnn_b0': _L1_gnn_in['b0'], 'L1_gnn_W1': _L1_gnn_in['W1'], 'L1_gnn_b1': _L1_gnn_in['b1']}

def reference(x, adj, L0_gnn_W, L0_gnn_b, L1_gnn_W0, L1_gnn_b0, L1_gnn_W1, L1_gnn_b1):
    import jax
    import jax.numpy as jnp

    def _L0_gnn_ref(x, adj, W, b):
        import jax, jax.numpy as jnp
        import numpy as np
        IN_DIM = 128
        OUT_DIM = 128
        N = 8192
        h_N = jnp.matmul(adj, x)
        h_cat = jnp.concatenate([x, h_N], axis=-1)
        out = jnp.maximum(jnp.einsum('nd,od->no', h_cat, W) + b, 0.0)
        return out

    def _L1_gnn_ref(x, L, W0, b0, W1, b1):
        import jax, jax.numpy as jnp
        import numpy as np
        N, D_IN, D_HID, D_OUT, K = (5000, 128, 128, 128, 3)

        def cheb_conv(x, L, W, b):
            Tx0 = x
            out = Tx0 @ W[0]
            Tx1 = L @ x
            out = out + Tx1 @ W[1]
            for k in range(2, W.shape[0]):
                Tx2 = 2.0 * (L @ Tx1) - Tx0
                out = out + Tx2 @ W[k]
                Tx0, Tx1 = (Tx1, Tx2)
            return out + b
        h = jax.nn.elu(cheb_conv(x, L, W0, b0))
        h = jax.nn.elu(cheb_conv(h, L, W1, b1))
        return h
    h = jnp.maximum(_layernorm(x, axis=-1), 0.0)
    x = x + _L0_gnn_ref(h, adj, L0_gnn_W, L0_gnn_b)
    h = jnp.maximum(_layernorm(x, axis=-1), 0.0)
    x = x + _L1_gnn_ref(h, adj, L1_gnn_W0, L1_gnn_b0, L1_gnn_W1, L1_gnn_b1)
    return x

_drawn_inputs = setup_inputs


def setup_inputs(seed=0):
    import zlib

    import numpy as np

    out = dict(_drawn_inputs(seed))
    spreads = {'L1_gnn_b0': (0.0, 0.649), 'L1_gnn_b1': (0.0, 0.8)}
    factors = {}
    for name, (base, spread) in spreads.items():
        noise = np.random.default_rng([zlib.crc32(name.encode()), seed]).standard_normal(out[name].shape)
        drawn = base * np.exp(spread * noise) if base else spread * noise
        out[name] = jnp.asarray(drawn.astype(out[name].dtype))
    for name, factor in factors.items():
        out[name] = (out[name] * factor).astype(out[name].dtype)
    return out
```

```python
from contextlib import ExitStack

import concourse.bass as bass
from concourse import mybir

F32 = mybir.dt.float32
F32R = mybir.dt.float32r
ALU = mybir.AluOpType
ACT = mybir.ActivationFunctionType

P = 128
N = 4096
BLOCKS = N // P
PANEL = 1024
PANELS = N // PANEL
TILE = 2 * PANEL
TILES = BLOCKS // 2
KEPT = TILES - 1
GROUP = 512
GROUPS = N // GROUP
RAW_SLOTS = 3
SPLIT_SLOTS = 2
EPS = 1e-5

AFTER = ["LN", "MID", "ELU", "MID", "LAST"]
W_SELF, W_NEIGH = 0, 1
W_ZERO = {0: 2, 1: 5}
W_ONE = {0: 3, 1: 6}
W_TWO = {0: 4, 1: 7}
WEIGHTS = 8


def pair_place(product, panel, g, again=0):
    if product < 0:
        return 2 * panel + g
    if product == 0:
        return GROUPS + 4 * panel + 2 * again + g
    return 3 * GROUPS + GROUPS * (product - 1) + 2 * panel + g


def build(nc, x, adj_tiles, w0t, w1, w2, b0, b1, b2, out):
    with ExitStack() as ctx:
        def sb(name, shape, dt=F32):
            return ctx.enter_context(nc.sbuf_tensor(name, shape, dt))

        def sem(name):
            return ctx.enter_context(nc.semaphore(name))

        s_hi = [sb(f"s_hi{i}", [P, N], F32R) for i in range(2)]
        s_lo = [sb(f"s_lo{i}", [P, N], F32R) for i in range(2)]
        rest = sb("rest", [P, N])
        xres = sb("xres", [P, N])
        raw = sb("raw", [P, RAW_SLOTS, TILE])
        kept = sb("kept", [P, PANELS * TILE])
        a_hi = sb("a_hi", [P, SPLIT_SLOTS, TILE], F32R)
        a_lo = sb("a_lo", [P, SPLIT_SLOTS, TILE], F32R)
        w_hi = sb("w_hi", [P, WEIGHTS, P], F32R)
        w_lo = sb("w_lo", [P, WEIGHTS, P], F32R)
        pair_hi = sb("pair_hi", [P, GROUP], F32R)
        pair_lo = sb("pair_lo", [P, GROUP], F32R)
        pre = sb("pre", [P, GROUP])
        expo = sb("expo", [P, GROUP])
        act_out = sb("act_out", [P, GROUP])
        ident = sb("ident", [P, P])
        bias0 = sb("bias0", [P, P])
        bias_col = sb("bias_col", [P, 2])
        eps = sb("eps", [P, 1])
        stats = sb("stats", [P, BLOCKS, 6])
        meanvar = sb("meanvar", [P, BLOCKS, 2])
        std = sb("std", [P, BLOCKS])
        rstd = sb("rstd", [P, BLOCKS])
        shift = sb("shift", [P, BLOCKS])

        sums = ctx.enter_context(nc.psum_tensor("sums", [P, 2 * PANEL], F32))
        small_a = [ctx.enter_context(nc.psum_tensor(f"small_a{i}", [P, GROUP], F32)) for i in range(2)]
        small_b = [ctx.enter_context(nc.psum_tensor(f"small_b{i}", [P, GROUP], F32)) for i in range(2)]

        x_loaded = [sem(f"x_loaded{i}") for i in range(4)]
        w_loaded = sem("w_loaded")
        bias_loaded = sem("bias_loaded")
        raw_loaded = [sem(f"raw_loaded{i}") for i in range(RAW_SLOTS)]
        kept_loaded = sem("kept_loaded")
        zeros_ready = sem("zeros_ready")
        ident_ready = sem("ident_ready")
        eps_ready = sem("eps_ready")
        w_sub = sem("w_sub")
        w_made = sem("w_made")
        w_hi_ready = sem("w_hi_ready")
        w_lo_ready = sem("w_lo_ready")
        hi_ready = sem("hi_ready")
        lo_ready = sem("lo_ready")
        tile_used = sem("tile_used")
        pair_hi_ready = sem("pair_hi_ready")
        pair_lo_ready = sem("pair_lo_ready")
        pair_used = sem("pair_used")
        stat_hi_ready = sem("stat_hi_ready")
        stat_lo_ready = sem("stat_lo_ready")
        rest_ready = sem("rest_ready")
        pre_ready = sem("pre_ready")
        res_ready = sem("res_ready")
        stats_ready = sem("stats_ready")
        meanvar_ready = sem("meanvar_ready")
        std_ready = sem("std_ready")
        rstd_ready = sem("rstd_ready")
        shift_ready = sem("shift_ready")
        neg_ready = sem("neg_ready")
        expo_ready = sem("expo_ready")
        norm_ready = sem("norm_ready")
        elu_ready = sem("elu_ready")
        turned = sem("turned")
        out_ready = sem("out_ready")
        stored = sem("stored")

        def tiles(product, panel, t):
            return (product * PANELS + panel) * TILES + t + 1

        def stat(product, k):
            return (product + 1) * GROUPS + k + 1

        rest_count = stat

        def norms(product, k):
            return (product + 1) * GROUPS + k + 1

        def elus(product, k):
            return 1 + (GROUPS if product == 4 else 0) + k + 1

        def residuals(k):
            return 1 + k + 1

        def turns(product, k):
            return {-1: 0, 0: 1, 2: 2, 4: 3}[product] * GROUPS + k + 1

        def cols(panel, g):
            return bass.ds(panel * PANEL + g * GROUP, GROUP)

        def sum_cols(panel, g):
            return bass.ds((panel % 2) * PANEL + g * GROUP, GROUP)

        def blk(b):
            return slice(b * P, (b + 1) * P)

        def kept_cols(panel):
            return bass.ds(panel * TILE, TILE)

        def conv(product):
            return 0 if product < 3 else 1

        block = ctx.enter_context(nc.Block())

        @block.sync
        def _(sp):
            def load(product, panel, t):
                if t >= RAW_SLOTS:
                    sp.wait_ge(lo_ready, tiles(product, panel, t - RAW_SLOTS))
                elif not (product == 0 and isinstance(panel, int)):
                    sp.wait_ge(lo_ready, tiles(product, panel - 1, t - RAW_SLOTS + KEPT))
                sp.dma_start(raw[:, t % RAW_SLOTS, :], adj_tiles[bass.ds(panel * TILES + t, 1), :, :]
                             ).then_inc(raw_loaded[t % RAW_SLOTS], 16)

            def load_kept(panel):
                if not isinstance(panel, int):
                    sp.wait_ge(kept_loaded, 16 * panel)
                sp.dma_start(kept[:, kept_cols(panel)], adj_tiles[bass.ds(panel * TILES + KEPT, 1), :, :]
                             ).then_inc(kept_loaded, 16)

            def store(panel):
                sp.wait_ge(out_ready, 2 * panel + 2)
                sp.dma_start(out[:, bass.ds(panel * PANEL, PANEL)],
                             xres[:, bass.ds(panel * PANEL, PANEL)]).then_inc(stored, 16)

            def panel_loads(product, panel, storing=False):
                for t in range(KEPT):
                    load(product, panel, t)
                    if storing and t == KEPT - 1:
                        store(panel - 1)
                if product == 0:
                    load_kept(panel)

            for i in range(4):
                sp.dma_start(xres[:, i * PANEL:(i + 1) * PANEL],
                             x[:, i * PANEL:(i + 1) * PANEL]).then_inc(x_loaded[i], 16)
            for product in range(5):
                panel_loads(product, 0)
                with sp.Fori(1, PANELS) as panel:
                    panel_loads(product, panel, storing=product == 4)
            store(PANELS - 1)
            sp.wait_ge(stored, 16 * PANELS)

        @block.gpsimd
        def _(pool):
            nc.gpsimd.memset(eps[:], EPS).then_inc(eps_ready, 1)
            nc.gpsimd.memset(expo[:], 0.0).then_inc(elu_ready, 1)
            nc.gpsimd.memset(pre[:], 0.0).then_inc(res_ready, 1)
            nc.gpsimd.memset(ident[:], 0.0).then_inc(zeros_ready, 1)
            pool.wait_ge(zeros_ready, 1)
            nc.gpsimd.affine_select(out=ident[:], in_=ident[:], compare_op=ALU.not_equal, fill=1.0,
                                    base=0, pattern=[[-1, P]], channel_multiplier=1
                                    ).then_inc(ident_ready, 1)

        @block.scalar
        def _(act):
            def split_hi(product, panel, t):
                if t == KEPT:
                    if product == 0:
                        act.wait_ge(kept_loaded, 16 * (panel + 1))
                    src = kept[:, kept_cols(panel)]
                else:
                    act.wait_ge(raw_loaded[t % RAW_SLOTS],
                                16 * ((product * PANELS + panel) * (KEPT // RAW_SLOTS) + t // RAW_SLOTS + 1))
                    src = raw[:, t % RAW_SLOTS, :]
                if not (product == 0 and isinstance(panel, int) and t < SPLIT_SLOTS):
                    act.wait_ge(tile_used, tiles(product, panel, t - SPLIT_SLOTS))
                nc.scalar.activation(a_hi[:, t % SPLIT_SLOTS, :], src, ACT.Copy).then_inc(hi_ready, 1)

            def sums_to_pair(product, panel, g):
                act.wait_ge(tile_used, tiles(product, panel, TILES - 1))
                act.wait_ge(pair_used, pair_place(product, panel, g))
                nc.scalar.activation(pair_hi[:], sums[:, sum_cols(panel, g)], ACT.Copy).then_inc(pair_hi_ready, 1)

            def norm_std(product, k, where):
                act.wait_ge(meanvar_ready, 1 if product < 0 else k + 2)
                if product < 0:
                    act.wait_ge(eps_ready, 1)
                nc.scalar.activation(std[:, where], meanvar[:, where, 1], ACT.Sqrt,
                                     bias=eps[:]).then_inc(std_ready, 1)

            def norm_apply(product, panel, g, first):
                k = 2 * panel + g
                act.wait_ge(shift_ready, 1 if product < 0 else k + 2)
                if not (product < 0 and k == 0):
                    act.wait_ge(turned, norms(product, k - 1))
                    act.wait_ge(stat_lo_ready, stat(product, k - 1))
                for b in range(4):
                    last = nc.scalar.activation(act_out[:, blk(b)],
                                                xres[:, bass.ds(panel * PANEL + (4 * g + b) * P, P)], ACT.Relu,
                                                bias=shift[:, first + b:first + b + 1],
                                                scale=rstd[:, first + b:first + b + 1])
                last.then_inc(norm_ready, 1)
                act.wait_ge(norm_ready, norms(product, k))
                nc.scalar.activation(s_hi[(product + 1) % 2][:, cols(panel, g)], act_out[:],
                                     ACT.Copy).then_inc(stat_hi_ready, 1)

            def turned_to_pair(product, panel, g):
                k = 2 * panel + g
                act.wait_ge(turned, turns(product, k))
                act.wait_ge(pair_used, pair_place(product, panel, g, 1))
                nc.scalar.activation(pair_hi[:], small_a[g][:], ACT.Copy).then_inc(pair_hi_ready, 1)

            def rest_from_product(product, panel, g):
                act.wait_ge(pair_used, pair_place(product, panel, g, 1) + 1)
                if product == 0:
                    act.wait_ge(bias_loaded, 48)
                c = 0 if product == 0 else 1
                nc.scalar.activation(rest[:, cols(panel, g)], small_b[g][:], ACT.Identity,
                                     bias=bias_col[:, c:c + 1]).then_inc(rest_ready, 1)

            def after(product, panel, slot):
                kind = AFTER[product]
                for g in range(2):
                    k = 2 * panel + g
                    if kind == "LN":
                        s = slot - 1 - 2 * g
                        if s == 0:
                            sums_to_pair(product, panel, g)
                        if s == 5:
                            norm_std(product, k, slice(4 * g, 4 * g + 4))
                        if s == 6:
                            norm_apply(product, panel, g, 4 * g)
                        if s == 8:
                            turned_to_pair(product, panel, g)
                        if s == 10:
                            rest_from_product(product, panel, g)
                    if kind == "MID":
                        s = slot - 1 - 2 * g
                        if s == 0:
                            sums_to_pair(product, panel, g)
                        if s == 2:
                            act.wait_ge(pair_used, pair_place(product, panel, g) + 1)
                            nc.scalar.activation(s_hi[(product + 1) % 2][:, cols(panel, g)], small_a[g][:],
                                                 ACT.Copy).then_inc(stat_hi_ready, 1)
                    if kind in ("ELU", "LAST"):
                        s = slot - 1 - 3 * g
                        if s == 1:
                            n = elus(product, k)
                            act.wait_ge(pre_ready, GROUPS + n - 1)
                            act.wait_ge(elu_ready, n - 1)
                            nc.scalar.activation(expo[:], pre[:], ACT.Relu, scale=-1.0).then_inc(neg_ready, 1)
                            act.wait_ge(neg_ready, n - 1)
                            nc.scalar.activation(expo[:], expo[:], ACT.Exp, scale=-1.0).then_inc(expo_ready, 1)
                    if kind == "ELU":
                        if s == 3:
                            act.wait_ge(turned, turns(product, k))
                            nc.scalar.activation(s_hi[(product + 1) % 2][:, cols(panel, g)], small_a[g][:],
                                                 ACT.Copy).then_inc(stat_hi_ready, 1)
                            act.wait_ge(pair_used, pair_place(product, panel, g))
                            nc.scalar.activation(pair_hi[:], act_out[:], ACT.Copy).then_inc(pair_hi_ready, 1)
                        if s == 5:
                            rest_from_product(product, panel, g)

            act.dma_start(rest[:, 0:2 * P], w0t).then_inc(w_loaded, 16)
            act.dma_start(rest[:, 2 * P:5 * P], w1).then_inc(w_loaded, 16)
            act.dma_start(rest[:, 5 * P:8 * P], w2).then_inc(w_loaded, 16)
            act.dma_start(bias0[:], b0).then_inc(bias_loaded, 16)
            act.dma_start(bias_col[:, 0:1], b1).then_inc(bias_loaded, 16)
            act.dma_start(bias_col[:, 1:2], b2).then_inc(bias_loaded, 16)
            act.wait_ge(w_made, 1)
            nc.scalar.activation(w_hi[:, :, :], rest[:, 0:WEIGHTS * P].rearrange("p (w n) -> p w n", n=P),
                                 ACT.Copy).then_inc(w_hi_ready, 1)
            norm_std(-1, 0, slice(0, BLOCKS))
            for t in range(TILES):
                if t % 2 == 0:
                    norm_apply(-1, t // 4, t // 2 % 2, 2 * t)
                split_hi(0, 0, t)
                if t % 2 == 1:
                    turned_to_pair(-1, t // 4, t // 2 % 2)
            for product in range(5):
                if product:
                    for t in range(TILES):
                        split_hi(product, 0, t)
                        after(product - 1, PANELS - 1, t)
                with act.Fori(1, PANELS) as panel:
                    for t in range(TILES):
                        split_hi(product, panel, t)
                        after(product, panel - 1, t)
            for t in range(TILES):
                after(4, PANELS - 1, t)

        @block.vector
        def _(dve):
            def split_lo(product, panel, t):
                dve.wait_ge(hi_ready, tiles(product, panel, t))
                src = kept[:, kept_cols(panel)] if t == KEPT else raw[:, t % RAW_SLOTS, :]
                nc.vector.tensor_tensor(a_lo[:, t % SPLIT_SLOTS, :], src,
                                        a_hi[:, t % SPLIT_SLOTS, :].bitcast(F32), ALU.subtract).then_inc(lo_ready, 1)

            def pair_low(product, panel, g, src, again=0):
                dve.wait_ge(pair_hi_ready, pair_place(product, panel, g, again) + 1)
                nc.vector.tensor_tensor(pair_lo[:], src, pair_hi[:].bitcast(F32),
                                        ALU.subtract).then_inc(pair_lo_ready, 1)

            def stat_low(product, panel, g, src):
                dve.wait_ge(stat_hi_ready, stat(product, 2 * panel + g))
                buf = (product + 1) % 2
                nc.vector.tensor_tensor(s_lo[buf][:, cols(panel, g)], src,
                                        s_hi[buf][:, cols(panel, g)].bitcast(F32),
                                        ALU.subtract).then_inc(stat_lo_ready, 1)

            def norm_scale(product, k, n, where):
                dve.wait_ge(std_ready, n)
                nc.vector.reciprocal(rstd[:, where], std[:, where]).then_inc(rstd_ready, 1)
                dve.wait_ge(rstd_ready, n)
                nc.vector.scalar_tensor_tensor(out=shift[:, where], in0=meanvar[:, where, 0], scalar=-1.0,
                                               in1=rstd[:, where], op0=ALU.mult, op1=ALU.mult
                                               ).then_inc(shift_ready, 1)

            def rest_opening(k):
                dve.wait_ge(pair_used, k + 1)
                if k == 0:
                    dve.wait_ge(bias_loaded, 48)
                for b in range(4):
                    last = nc.vector.tensor_tensor(rest[:, k * GROUP + b * P:k * GROUP + (b + 1) * P],
                                                   small_b[k % 2][:, blk(b)], bias0[:], ALU.add)
                last.then_inc(rest_ready, 1)

            def ahead(product, panel, slot):
                for g in range(2):
                    k = 2 * panel + g
                    s = slot - 1 - 2 * g
                    if AFTER[product] == "LN" and s == 3:
                        dve.wait_ge(res_ready, residuals(k))
                    if AFTER[product] == "LN" and s == 4:
                        dve.wait_ge(stats_ready, k + 2)

            def after(product, panel, slot):
                kind = AFTER[product]
                for g in range(2):
                    k = 2 * panel + g
                    if kind == "LN":
                        s = slot - 1 - 2 * g
                        if s == 0:
                            pair_low(product, panel, g, sums[:, sum_cols(panel, g)])
                        if s == 2:
                            dve.wait_ge(pair_used, pair_place(product, panel, g) + 1)
                            dve.wait_ge(rest_ready, rest_count(-1, k))
                            dve.wait_ge(res_ready, residuals(k) - 1)
                            nc.vector.tensor_tensor(pre[:], small_a[g][:], rest[:, cols(panel, g)],
                                                    ALU.add).then_inc(pre_ready, 1)
                            dve.wait_ge(pre_ready, k + 1)
                            nc.vector.scalar_tensor_tensor(out=xres[:, cols(panel, g)], in0=pre[:], scalar=0.0,
                                                           in1=xres[:, cols(panel, g)], op0=ALU.max,
                                                           op1=ALU.add).then_inc(res_ready, 1)
                        if s == 3:
                            for b in range(4):
                                last = nc.vector.bn_stats(stats[:, 4 * g + b, :],
                                                          xres[:, bass.ds(panel * PANEL + (4 * g + b) * P, P)])
                            last.then_inc(stats_ready, 1)
                        if s == 4:
                            for b in range(4):
                                last = nc.vector.bn_aggr(meanvar[:, 4 * g + b, :], stats[:, 4 * g + b, :])
                            last.then_inc(meanvar_ready, 1)
                        if s == 5:
                            norm_scale(product, k, k + 2, slice(4 * g, 4 * g + 4))
                        if s == 6:
                            stat_low(product, panel, g, act_out[:])
                        if s == 8:
                            pair_low(product, panel, g, small_a[g][:], 1)
                    if kind == "MID":
                        s = slot - 1 - 2 * g
                        if s == 0:
                            pair_low(product, panel, g, sums[:, sum_cols(panel, g)])
                        if s == 2:
                            stat_low(product, panel, g, small_a[g][:])
                        if s == 3:
                            dve.wait_ge(rest_ready, rest_count(product - 1, k))
                            dve.wait_ge(pair_used, pair_place(product, panel, g) + 1)
                            nc.vector.tensor_tensor(rest[:, cols(panel, g)], small_b[g][:], rest[:, cols(panel, g)],
                                                    ALU.add).then_inc(rest_ready, 1)
                    if kind in ("ELU", "LAST"):
                        s = slot - 1 - 3 * g
                        n = elus(product, k)
                        if s == 0:
                            dve.wait_ge(tile_used, tiles(product, panel, TILES - 1))
                            dve.wait_ge(rest_ready, rest_count(product - 1, k))
                            dve.wait_ge(elu_ready, n - 1)
                            nc.vector.tensor_tensor(pre[:], sums[:, sum_cols(panel, g)], rest[:, cols(panel, g)],
                                                    ALU.add).then_inc(pre_ready, 1)
                        if s == 2:
                            dve.wait_ge(expo_ready, n - 1)
                            dve.wait_ge(turned, turns(product, k) - 1)
                            dve.wait_ge(pair_hi_ready, pair_place(min(product, 3), panel, g)
                                        if product == 2 else pair_place(3, PANELS - 1, 1) + 1)
                            nc.vector.scalar_tensor_tensor(out=act_out[:], in0=expo[:], scalar=1.0, in1=pre[:],
                                                           op0=ALU.subtract, op1=ALU.max).then_inc(elu_ready, 1)
                    if kind == "ELU" and s == 3:
                        stat_low(product, panel, g, small_a[g][:])
                        pair_low(product, panel, g, act_out[:])
                    if kind == "LAST" and s == 4:
                        dve.wait_ge(turned, turns(product, k))
                        nc.vector.tensor_tensor(xres[:, cols(panel, g)], small_a[g][:], xres[:, cols(panel, g)],
                                                ALU.add).then_inc(out_ready, 1)

            for i in range(BLOCKS):
                if i % 8 == 0:
                    dve.wait_ge(x_loaded[i // 8], 16)
                last = nc.vector.bn_stats(stats[:, i, :], xres[:, i * P:(i + 1) * P])
            last.then_inc(stats_ready, 1)
            dve.wait_ge(stats_ready, 1)
            for i in range(BLOCKS):
                last = nc.vector.bn_aggr(meanvar[:, i, :], stats[:, i, :])
            last.then_inc(meanvar_ready, 1)
            dve.wait_ge(w_loaded, 48)
            raw_w = rest[:, 0:WEIGHTS * P].rearrange("p (w n) -> p w n", n=P)
            for c in range(2):
                last = nc.vector.tensor_tensor(raw_w[:, W_ZERO[c], :], raw_w[:, W_ZERO[c], :],
                                               raw_w[:, W_TWO[c], :], ALU.subtract)
            last.then_inc(w_sub, 1)
            dve.wait_ge(w_sub, 1)
            for c in range(2):
                last = nc.vector.tensor_scalar(raw_w[:, W_TWO[c], :], raw_w[:, W_TWO[c], :], 2.0, None, ALU.mult)
            last.then_inc(w_made, 1)
            norm_scale(-1, 0, 1, slice(0, BLOCKS))
            dve.wait_ge(w_hi_ready, 1)
            nc.vector.tensor_tensor(w_lo[:, :, :], raw_w, w_hi[:, :, :].bitcast(F32),
                                    ALU.subtract).then_inc(w_lo_ready, 1)
            for t in range(TILES):
                if t % 2 == 0:
                    stat_low(-1, t // 4, t // 2 % 2, act_out[:])
                split_lo(0, 0, t)
                if t % 2 == 1:
                    if t >= 3:
                        rest_opening(t // 2 - 1)
                    pair_low(-1, t // 4, t // 2 % 2, small_a[t // 2 % 2][:])
            rest_opening(GROUPS - 1)
            for product in range(5):
                if product:
                    for t in range(TILES):
                        ahead(product - 1, PANELS - 1, t)
                        split_lo(product, 0, t)
                        after(product - 1, PANELS - 1, t)
                with dve.Fori(1, PANELS) as panel:
                    for t in range(TILES):
                        ahead(product, panel - 1, t)
                        split_lo(product, panel, t)
                        after(product, panel - 1, t)
            for t in range(TILES):
                after(4, PANELS - 1, t)

        @block.tensor
        def _(pe):
            def multiply(product, panel, t):
                buf = product % 2
                if isinstance(panel, int):
                    pe.wait_ge(stat_lo_ready, stat(product - 1, t // 2))
                slot = t % SPLIT_SLOTS

                def part(weights, moving, jj, start=False, stop=False):
                    j = 2 * t + jj
                    for g in range(2):
                        last = nc.tensor.matmul(sums[:, sum_cols(panel, g)], weights[:, blk(j)],
                                                moving[:, slot, jj * PANEL + g * GROUP:jj * PANEL + (g + 1) * GROUP],
                                                start=start, stop=stop)
                    return last

                pe.wait_ge(hi_ready, tiles(product, panel, t))
                for jj in range(2):
                    part(s_hi[buf], a_hi, jj, start=(t == 0 and jj == 0))
                    part(s_lo[buf], a_hi, jj)
                pe.wait_ge(lo_ready, tiles(product, panel, t))
                for jj in range(2):
                    last = part(s_hi[buf], a_lo, jj, stop=(t == TILES - 1 and jj == 1))
                last.then_inc(tile_used, 1)

            def pair_rows(dst, w):
                for b in range(4):
                    nc.tensor.matmul(dst[:, blk(b)], pair_hi[:, blk(b)], w_hi[:, w, :], start=True, stop=False)
                    nc.tensor.matmul(dst[:, blk(b)], pair_lo[:, blk(b)], w_hi[:, w, :], start=False, stop=False)
                    last = nc.tensor.matmul(dst[:, blk(b)], pair_hi[:, blk(b)], w_lo[:, w, :], start=False, stop=True)
                return last

            def pair_columns(dst, w):
                nc.tensor.matmul(dst[:], w_hi[:, w, :], pair_hi[:], start=True, stop=False)
                nc.tensor.matmul(dst[:], w_lo[:, w, :], pair_hi[:], start=False, stop=False)
                return nc.tensor.matmul(dst[:], w_hi[:, w, :], pair_lo[:], start=False, stop=True)

            def turn(dst):
                for b in range(4):
                    last = nc.tensor.transpose(dst[:, blk(b)], act_out[:, blk(b)], ident[:])
                last.then_inc(turned, 1)

            def after(product, panel, slot):
                kind = AFTER[product]
                for g in range(2):
                    k = 2 * panel + g
                    if kind == "LN":
                        s = slot - 1 - 2 * g
                        if s == 0:
                            pe.wait_ge(pair_lo_ready, pair_place(product, panel, g) + 1)
                            pair_rows(small_a[g], W_NEIGH).then_inc(pair_used, 1)
                        if s == 6:
                            pe.wait_ge(norm_ready, norms(product, k))
                            pe.wait_ge(pre_ready, k + 1)
                            turn(small_a[g])
                        if s == 8:
                            pe.wait_ge(pair_lo_ready, pair_place(product, panel, g, 1) + 1)
                            pe.wait_ge(rest_ready, rest_count(product, k) - 2)
                            pair_columns(small_b[g], W_ZERO[0]).then_inc(pair_used, 1)
                    if kind == "MID":
                        s = slot - 1 - 2 * g
                        if s == 0:
                            pe.wait_ge(pair_lo_ready, pair_place(product, panel, g) + 1)
                            pe.wait_ge(stat_lo_ready, stat(product, k) - 2)
                            pe.wait_ge(rest_ready, rest_count(product, k) - 2)
                            pair_rows(small_a[g], W_TWO[conv(product)])
                            pair_columns(small_b[g], W_ONE[conv(product)]).then_inc(pair_used, 1)
                    if kind in ("ELU", "LAST"):
                        s = slot - 1 - 3 * g
                        if s == 2:
                            pe.wait_ge(elu_ready, elus(product, k))
                            if product == 2:
                                pe.wait_ge(stat_lo_ready, stat(product, k) - 2)
                            turn(small_a[g])
                    if kind == "ELU" and s == 3:
                        pe.wait_ge(pair_lo_ready, pair_place(product, panel, g) + 1)
                        pe.wait_ge(rest_ready, rest_count(product, k) - 2)
                        pair_columns(small_b[g], W_ZERO[1]).then_inc(pair_used, 1)

            pe.wait_ge(ident_ready, 1)
            for t in range(TILES):
                k = t // 2
                if t % 2 == 0:
                    pe.wait_ge(norm_ready, k + 1)
                    if k >= 2:
                        pe.wait_ge(pair_lo_ready, k - 1)
                    turn(small_a[k % 2])
                multiply(0, 0, t)
                if t % 2 == 1:
                    if k == 0:
                        pe.wait_ge(w_lo_ready, 1)
                    pe.wait_ge(pair_lo_ready, k + 1)
                    if k >= 2:
                        pe.wait_ge(rest_ready, k - 1)
                    pair_rows(small_b[k % 2], W_SELF).then_inc(pair_used, 1)
            for product in range(5):
                if product:
                    for t in range(TILES):
                        multiply(product, 0, t)
                        after(product - 1, PANELS - 1, t)
                with pe.Fori(1, PANELS) as panel:
                    for t in range(TILES):
                        multiply(product, panel, t)
                        after(product, panel - 1, t)
            for t in range(TILES):
                after(4, PANELS - 1, t)


def kernel(**inputs):
    import numpy as np
    import concourse.bacc as bacc
    from concourse import mybir as mb
    from concourse.bass_utils import run_bass_kernel_spmd

    a = {k: np.asarray(v) for k, v in inputs.items()}

    def rows(m):
        return np.ascontiguousarray(m.reshape(-1, P, P).transpose(1, 0, 2).reshape(P, -1))

    tiles = a["adj"].reshape(PANELS, PANEL, TILES, 2, P).transpose(0, 2, 4, 3, 1)
    arrays = {
        "x": rows(a["x"]),
        "adj_tiles": np.ascontiguousarray(tiles).reshape(PANELS * TILES, P, TILE),
        "w0t": rows(a["L0_gnn_W"].T),
        "w1": rows(a["L1_gnn_W0"].reshape(-1, P)),
        "w2": rows(a["L1_gnn_W1"].reshape(-1, P)),
        "b0": np.ascontiguousarray(np.broadcast_to(a["L0_gnn_b"], (P, P))),
        "b1": a["L1_gnn_b0"].reshape(P, 1),
        "b2": a["L1_gnn_b1"].reshape(P, 1),
    }
    nc = bacc.Bacc("TRN2", target_bir_lowering=False, num_devices=1)
    args = [nc.dram_tensor(f"in_{k}", v.shape, mb.dt.from_np(v.dtype), kind="ExternalInput").ap()
            for k, v in arrays.items()]
    out = nc.dram_tensor("out", (P, N), F32, kind="ExternalOutput").ap()
    build(nc, *args, out)
    r = run_bass_kernel_spmd(nc, [{f"in_{k}": v for k, v in arrays.items()}], core_ids=[0])
    got = r.results[0]["out"]
    return np.ascontiguousarray(got.reshape(P, BLOCKS, P).transpose(1, 0, 2)).reshape(N, P)
```

```python
from contextlib import ExitStack

import concourse.bass as bass
from concourse import mybir

F32 = mybir.dt.float32
F32R = mybir.dt.float32r
ALU = mybir.AluOpType
ACT = mybir.ActivationFunctionType

P = 128
N = 4096
BLOCKS = N // P
PANEL = 1024
PANELS = N // PANEL
TILES = BLOCKS
KEPT = 15
KEPT_TILES = 2
LOADED = TILES - KEPT_TILES
GROUP = 512
GROUPS = N // GROUP
RAW_SLOTS = 6
SPLIT_SLOTS = 4
EPS = 1e-5
LAG = 2
STAGGER = 5

AFTER = ["LN", "MID", "ELU", "MID", "LAST"]
W_SELF, W_NEIGH = 0, 1
W_ZERO = {0: 2, 1: 5}
W_ONE = {0: 3, 1: 6}
W_TWO = {0: 4, 1: 7}
WEIGHTS = 8




def forward(product, first):
    return first if product == 0 else product % 2 == 1


def tile_at(product, first, i):
    return i if forward(product, first) else TILES - 1 - i


def panel_at(product, step):
    return step if product % 2 == 0 else (3 * step + 3) & 3


def half_at(product, g):
    return g if product % 2 == 0 else 1 - g


def slot_at(product, n, slots):
    return n % slots if product % 2 == 0 else slots - 1 - n % slots


def place_of(q):
    return q if q < KEPT else q + KEPT_TILES


def pair_place(product, panel, g, again=0):
    if product < 0:
        return 2 * panel + g
    if product == 0:
        return GROUPS + 4 * panel + 2 * again + g
    return 3 * GROUPS + GROUPS * (product - 1) + 2 * panel + g


def build(nc, x, adj_tiles, w0t, w1, w2, b0, b1, b2, out):
    with ExitStack() as ctx:
        def sb(name, shape, dt=F32):
            return ctx.enter_context(nc.sbuf_tensor(name, shape, dt))

        def sem(name):
            return ctx.enter_context(nc.semaphore(name))

        s_hi = [sb(f"s_hi{i}", [P, N], F32R) for i in range(2)]
        s_lo = [sb(f"s_lo{i}", [P, N], F32R) for i in range(2)]
        rest = sb("rest", [P, N])
        xres = sb("xres", [P, N])
        raw = sb("raw", [P, RAW_SLOTS, PANEL])
        kept = sb("kept", [P, PANELS * KEPT_TILES * PANEL])
        a_hi = sb("a_hi", [P, SPLIT_SLOTS, PANEL], F32R)
        a_lo = sb("a_lo", [P, SPLIT_SLOTS, PANEL], F32R)
        w_hi = sb("w_hi", [P, WEIGHTS, P], F32R)
        w_lo = sb("w_lo", [P, WEIGHTS, P], F32R)
        pair_hi = sb("pair_hi", [P, GROUP], F32R)
        pair_lo = sb("pair_lo", [P, GROUP], F32R)
        pre = sb("pre", [P, GROUP])
        expo = sb("expo", [P, GROUP])
        act_out = sb("act_out", [P, GROUP])
        ident = sb("ident", [P, P])
        bias0 = sb("bias0", [P, P])
        bias_col = sb("bias_col", [P, 2])
        eps = sb("eps", [P, 1])
        stats = sb("stats", [P, BLOCKS, 6])
        meanvar = sb("meanvar", [P, BLOCKS, 2])
        std = sb("std", [P, BLOCKS])
        rstd = sb("rstd", [P, BLOCKS])
        shift = sb("shift", [P, BLOCKS])

        sums = ctx.enter_context(nc.psum_tensor("sums", [P, 2 * PANEL], F32))
        small_a = [ctx.enter_context(nc.psum_tensor(f"small_a{i}", [P, GROUP], F32)) for i in range(2)]
        small_b = [ctx.enter_context(nc.psum_tensor(f"small_b{i}", [P, GROUP], F32)) for i in range(2)]

        x_loaded = [sem(f"x_loaded{i}") for i in range(GROUPS)]
        w_loaded = sem("w_loaded")
        bias_loaded = sem("bias_loaded")
        raw_loaded = [sem(f"raw_loaded{i}") for i in range(RAW_SLOTS)]
        kept_loaded = sem("kept_loaded")
        zeros_ready = sem("zeros_ready")
        ident_ready = sem("ident_ready")
        eps_ready = sem("eps_ready")
        w_sub = sem("w_sub")
        w_made = sem("w_made")
        w_hi_ready = sem("w_hi_ready")
        w_lo_ready = sem("w_lo_ready")
        hi_ready = sem("hi_ready")
        lo_ready = sem("lo_ready")
        tile_used = sem("tile_used")
        pair_hi_ready = sem("pair_hi_ready")
        pair_lo_ready = sem("pair_lo_ready")
        pair_used = sem("pair_used")
        stat_hi_ready = sem("stat_hi_ready")
        stat_lo_ready = sem("stat_lo_ready")
        rest_ready = sem("rest_ready")
        pre_ready = sem("pre_ready")
        res_ready = sem("res_ready")
        stats_ready = sem("stats_ready")
        meanvar_ready = sem("meanvar_ready")
        std_ready = sem("std_ready")
        rstd_ready = sem("rstd_ready")
        shift_ready = sem("shift_ready")
        neg_ready = sem("neg_ready")
        expo_ready = sem("expo_ready")
        norm_ready = sem("norm_ready")
        elu_ready = sem("elu_ready")
        turned = sem("turned")
        out_ready = sem("out_ready")
        stored = sem("stored")

        def used(product, step, i):
            return (product * PANELS + step) * TILES + i + 1

        def splits(product, step, i):
            return used(product, step, i) - SPLIT_SLOTS * product

        def splits_before(product):
            return splits(product - 1, PANELS - 1, TILES - 1)

        def loads(product, step, q):
            return (LOADED // RAW_SLOTS * PANELS - 1) * product + LOADED // RAW_SLOTS * step + q // RAW_SLOTS + 1

        def stat(product, k):
            return (product + 1) * GROUPS + k + 1

        rest_count = stat

        def norms(product, k):
            return (product + 1) * GROUPS + k + 1

        def elus(product, k):
            return 1 + (GROUPS if product == 4 else 0) + k + 1

        def residuals(k):
            return 1 + k + 1

        def turns(product, k):
            return {-1: 0, 0: 1, 2: 2, 4: 3}[product] * GROUPS + k + 1

        def cols(product, step, g):
            return bass.ds(panel_at(product, step) * PANEL + half_at(product, g) * GROUP, GROUP)

        def sum_cols(step, half):
            return bass.ds((step % 2) * PANEL + half * GROUP, GROUP)

        def blk(b):
            return slice(b * P, (b + 1) * P)

        def source(product, first, step, i):
            t = tile_at(product, first, i)
            if KEPT <= t < KEPT + KEPT_TILES:
                return kept[:, bass.ds((panel_at(product, step) * KEPT_TILES + t - KEPT) * PANEL, PANEL)]
            return raw[:, slot_at(product, i if i < KEPT else i - KEPT_TILES, RAW_SLOTS), :]

        def conv(product):
            return 0 if product < 3 else 1

        block = ctx.enter_context(nc.Block())

        @block.sync
        def _(sp):
            def load(product, first, step, q):
                if q >= RAW_SLOTS:
                    before = place_of(q - RAW_SLOTS)
                    if product and first and before < SPLIT_SLOTS:
                        sp.wait_ge(lo_ready, splits_before(product))
                    else:
                        sp.wait_ge(lo_ready, splits(product, step, before))
                elif not first:
                    sp.wait_ge(lo_ready, splits(product, step - 1, place_of(q + LOADED - RAW_SLOTS)))
                t = tile_at(product, first, place_of(q))
                slot = slot_at(product, q, RAW_SLOTS)
                sp.dma_start(raw[:, slot, :], adj_tiles[bass.ds(panel_at(product, step) * TILES + t, 1), :, :]
                             ).then_inc(raw_loaded[slot], 16)

            def load_kept(first, step):
                if not first:
                    sp.wait_ge(kept_loaded, 16 * step)
                sp.dma_start(kept[:, bass.ds(step * KEPT_TILES * PANEL, KEPT_TILES * PANEL)
                                  ].rearrange("p (t n) -> p t n", n=PANEL),
                             adj_tiles[bass.ds(step * TILES + KEPT, KEPT_TILES), :, :].rearrange("t p n -> p t n")
                             ).then_inc(kept_loaded, 16)

            def load_x(k):
                sp.dma_start(xres[:, k * GROUP:(k + 1) * GROUP],
                             x[:, k * GROUP:(k + 1) * GROUP]).then_inc(x_loaded[k], 16)

            def store(step):
                sp.wait_ge(out_ready, 2 * step + 2)
                sp.dma_start(out[:, bass.ds(step * PANEL, PANEL)],
                             xres[:, bass.ds(step * PANEL, PANEL)]).then_inc(stored, 16)

            def panel_loads(product, first, step):
                for q in range(RAW_SLOTS if product and first else 0, LOADED):
                    load(product, first, step, q)
                    if product == 0 and first and q % 4 == 0 and q // 4 + 2 < GROUPS:
                        load_x(q // 4 + 2)
                    if product == 0 and q == KEPT - RAW_SLOTS:
                        load_kept(first, step)
                    if product == 4 and not first and q == LOADED - RAW_SLOTS:
                        store(step - 1)

            load_x(0)
            load_x(1)
            for product in range(5):
                panel_loads(product, True, 0)
                with sp.Fori(1, PANELS) as step:
                    panel_loads(product, False, step)
            store(PANELS - 1)
            sp.wait_ge(stored, 16 * PANELS)

        @block.gpsimd
        def _(pool):
            nc.gpsimd.memset(eps[:], EPS).then_inc(eps_ready, 1)
            nc.gpsimd.memset(expo[:], 0.0).then_inc(elu_ready, 1)
            nc.gpsimd.memset(pre[:], 0.0).then_inc(res_ready, 1)
            nc.gpsimd.memset(ident[:], 0.0).then_inc(zeros_ready, 1)
            pool.wait_ge(zeros_ready, 1)
            nc.gpsimd.affine_select(out=ident[:], in_=ident[:], compare_op=ALU.not_equal, fill=1.0,
                                    base=0, pattern=[[-1, P]], channel_multiplier=1
                                    ).then_inc(ident_ready, 1)

        @block.scalar
        def _(act):
            def split_hi(product, first, step, i):
                if product and first and i < SPLIT_SLOTS:
                    return
                t = tile_at(product, first, i)
                if KEPT <= t < KEPT + KEPT_TILES:
                    if product == 0:
                        act.wait_ge(kept_loaded, 16 * (step + 1))
                else:
                    q = i if i < KEPT else i - KEPT_TILES
                    if not (product and first and q < RAW_SLOTS):
                        act.wait_ge(raw_loaded[slot_at(product, q, RAW_SLOTS)], 16 * loads(product, step, q))
                if not (product == 0 and first and i < SPLIT_SLOTS):
                    act.wait_ge(tile_used, used(product, step, i - SPLIT_SLOTS))
                nc.scalar.activation(a_hi[:, slot_at(product, i, SPLIT_SLOTS), :], source(product, first, step, i),
                                     ACT.Copy).then_inc(hi_ready, 1)

            def sums_to_pair(product, step, g):
                act.wait_ge(tile_used, used(product, step, TILES - 1))
                act.wait_ge(pair_used, pair_place(product, step, g))
                nc.scalar.activation(pair_hi[:], sums[:, sum_cols(step, half_at(product, g))],
                                     ACT.Copy).then_inc(pair_hi_ready, 1)

            def norm_std(n, first):
                act.wait_ge(meanvar_ready, n)
                nc.scalar.activation(std[:, first:first + 4], meanvar[:, first:first + 4, 1], ACT.Sqrt,
                                     bias=eps[:]).then_inc(std_ready, 1)

            def norm_apply(product, step, g, first):
                k = 2 * step + g
                act.wait_ge(shift_ready, norms(product, k))
                if not (product < 0 and k == 0):
                    act.wait_ge(turned, norms(product, k - 1))
                    act.wait_ge(stat_lo_ready, stat(product, k - 1))
                for b in range(4):
                    last = nc.scalar.activation(act_out[:, blk(b)],
                                                xres[:, bass.ds(step * PANEL + (4 * g + b) * P, P)], ACT.Relu,
                                                bias=shift[:, first + b:first + b + 1],
                                                scale=rstd[:, first + b:first + b + 1])
                last.then_inc(norm_ready, 1)
                act.wait_ge(norm_ready, norms(product, k))
                nc.scalar.activation(s_hi[(product + 1) % 2][:, cols(0, step, g)], act_out[:],
                                     ACT.Copy).then_inc(stat_hi_ready, 1)

            def turned_to_pair(product, step, g):
                act.wait_ge(turned, turns(product, 2 * step + g))
                act.wait_ge(pair_used, pair_place(product, step, g, 1))
                nc.scalar.activation(pair_hi[:], small_a[g][:], ACT.Copy).then_inc(pair_hi_ready, 1)

            def stat_high(product, step, g):
                nc.scalar.activation(s_hi[(product + 1) % 2][:, cols(product, step, g)], small_a[g][:],
                                     ACT.Copy).then_inc(stat_hi_ready, 1)

            def rest_from_product(product, step, g):
                act.wait_ge(pair_used, pair_place(product, step, g, 1) + 1)
                if product == 0:
                    act.wait_ge(bias_loaded, 48)
                c = 0 if product == 0 else 1
                nc.scalar.activation(rest[:, cols(product, step, g)], small_b[g][:], ACT.Identity,
                                     bias=bias_col[:, c:c + 1]).then_inc(rest_ready, 1)

            def after(product, step, i):
                kind = AFTER[product]
                for g in range(2):
                    k = 2 * step + g
                    s = i - LAG - STAGGER * g
                    if kind in ("LN", "MID") and s == 0:
                        sums_to_pair(product, step, g)
                    if kind == "LN" and s == 9:
                        norm_std(norms(0, k), 4 * g)
                    if kind == "LN" and s == 12:
                        norm_apply(product, step, g, 4 * g)
                    if kind == "LN" and s == 15:
                        turned_to_pair(product, step, g)
                    if kind == "LN" and s == 19:
                        rest_from_product(product, step, g)
                    if kind == "MID" and s == 4:
                        act.wait_ge(pair_used, pair_place(product, step, g) + 1)
                        stat_high(product, step, g)
                    if kind in ("ELU", "LAST") and s == 1:
                        n = elus(product, k)
                        act.wait_ge(pre_ready, GROUPS + n - 1)
                        act.wait_ge(elu_ready, n - 1)
                        nc.scalar.activation(expo[:], pre[:], ACT.Relu, scale=-1.0).then_inc(neg_ready, 1)
                        act.wait_ge(neg_ready, n - 1)
                        nc.scalar.activation(expo[:], expo[:], ACT.Exp, scale=-1.0).then_inc(expo_ready, 1)
                    if kind == "ELU" and s == 6:
                        act.wait_ge(turned, turns(product, k))
                        stat_high(product, step, g)
                    if kind == "ELU" and s == 7:
                        act.wait_ge(pair_used, pair_place(product, step, g))
                        nc.scalar.activation(pair_hi[:], act_out[:], ACT.Copy).then_inc(pair_hi_ready, 1)
                    if kind == "ELU" and s == 11:
                        rest_from_product(product, step, g)

            act.dma_start(rest[:, 0:2 * P], w0t).then_inc(w_loaded, 16)
            act.dma_start(rest[:, 2 * P:5 * P], w1).then_inc(w_loaded, 16)
            act.dma_start(rest[:, 5 * P:8 * P], w2).then_inc(w_loaded, 16)
            act.dma_start(bias0[:], b0).then_inc(bias_loaded, 16)
            act.dma_start(bias_col[:, 0:1], b1).then_inc(bias_loaded, 16)
            act.dma_start(bias_col[:, 1:2], b2).then_inc(bias_loaded, 16)
            act.wait_ge(eps_ready, 1)
            norm_std(1, 0)
            for i in range(TILES):
                k, r = i // 4, i % 4
                if r == 0:
                    norm_apply(-1, k // 2, k % 2, 4 * k)
                split_hi(0, True, 0, i)
                if i == 0:
                    act.wait_ge(w_made, 1)
                    nc.scalar.activation(w_hi[:, :, :], rest[:, 0:WEIGHTS * P].rearrange("p (w n) -> p w n", n=P),
                                         ACT.Copy).then_inc(w_hi_ready, 1)
                if r == 1:
                    turned_to_pair(-1, k // 2, k % 2)
                if r == 2 and k + 1 < GROUPS:
                    norm_std(k + 2, 4 * k + 4)
            for product in range(5):
                if product:
                    for i in range(TILES):
                        split_hi(product, True, 0, i)
                        after(product - 1, PANELS - 1, i)
                with act.Fori(1, PANELS) as step:
                    for i in range(TILES):
                        split_hi(product, False, step, i)
                        after(product, step - 1, i)
            for i in range(TILES):
                after(4, PANELS - 1, i)

        @block.vector
        def _(dve):
            def split_lo(product, first, step, i):
                if product and first and i < SPLIT_SLOTS:
                    return
                dve.wait_ge(hi_ready, splits(product, step, i))
                slot = slot_at(product, i, SPLIT_SLOTS)
                nc.vector.tensor_tensor(a_lo[:, slot, :], source(product, first, step, i),
                                        a_hi[:, slot, :].bitcast(F32), ALU.subtract).then_inc(lo_ready, 1)

            def pair_low(product, step, g, src, again=0):
                dve.wait_ge(pair_hi_ready, pair_place(product, step, g, again) + 1)
                nc.vector.tensor_tensor(pair_lo[:], src, pair_hi[:].bitcast(F32),
                                        ALU.subtract).then_inc(pair_lo_ready, 1)

            def stat_low(product, step, g, src):
                dve.wait_ge(stat_hi_ready, stat(product, 2 * step + g))
                buf, where = (product + 1) % 2, cols(max(product, 0), step, g)
                nc.vector.tensor_tensor(s_lo[buf][:, where], src, s_hi[buf][:, where].bitcast(F32),
                                        ALU.subtract).then_inc(stat_lo_ready, 1)

            def norm_stats(step, g, first):
                for b in range(4):
                    last = nc.vector.bn_stats(stats[:, first + b, :],
                                              xres[:, bass.ds(step * PANEL + (4 * g + b) * P, P)])
                last.then_inc(stats_ready, 1)

            def norm_meanvar(first):
                for b in range(4):
                    last = nc.vector.bn_aggr(meanvar[:, first + b, :], stats[:, first + b, :])
                last.then_inc(meanvar_ready, 1)

            def norm_scale(n, first):
                where = slice(first, first + 4)
                dve.wait_ge(std_ready, n)
                nc.vector.reciprocal(rstd[:, where], std[:, where]).then_inc(rstd_ready, 1)
                dve.wait_ge(rstd_ready, n)
                nc.vector.scalar_tensor_tensor(out=shift[:, where], in0=meanvar[:, where, 0], scalar=-1.0,
                                               in1=rstd[:, where], op0=ALU.mult, op1=ALU.mult
                                               ).then_inc(shift_ready, 1)

            def rest_opening(k):
                dve.wait_ge(pair_used, k + 1)
                if k == 0:
                    dve.wait_ge(bias_loaded, 48)
                for b in range(4):
                    last = nc.vector.tensor_tensor(rest[:, k * GROUP + b * P:k * GROUP + (b + 1) * P],
                                                   small_b[k % 2][:, blk(b)], bias0[:], ALU.add)
                last.then_inc(rest_ready, 1)

            def ahead(product, step, i):
                for g in range(2):
                    k = 2 * step + g
                    s = i - LAG - STAGGER * g
                    if AFTER[product] == "LN" and s == 6:
                        dve.wait_ge(res_ready, residuals(k))
                    if AFTER[product] == "LN" and s == 8:
                        dve.wait_ge(stats_ready, norms(0, k))

            def after(product, step, i):
                kind = AFTER[product]
                for g in range(2):
                    k = 2 * step + g
                    s = i - LAG - STAGGER * g
                    here = cols(product, step, g)
                    panel_sums = sums[:, sum_cols(step, half_at(product, g))]
                    if kind in ("LN", "MID") and s == 0:
                        pair_low(product, step, g, panel_sums)
                    if kind == "LN" and s == 4:
                        dve.wait_ge(pair_used, pair_place(product, step, g) + 1)
                        dve.wait_ge(rest_ready, GROUPS)
                        dve.wait_ge(res_ready, residuals(k) - 1)
                        nc.vector.tensor_tensor(pre[:], small_a[g][:], rest[:, here], ALU.add).then_inc(pre_ready, 1)
                        dve.wait_ge(pre_ready, k + 1)
                        nc.vector.scalar_tensor_tensor(out=xres[:, here], in0=pre[:], scalar=0.0,
                                                       in1=xres[:, here], op0=ALU.max,
                                                       op1=ALU.add).then_inc(res_ready, 1)
                    if kind == "LN" and s == 6:
                        norm_stats(step, g, 4 * g)
                    if kind == "LN" and s == 8:
                        norm_meanvar(4 * g)
                    if kind == "LN" and s == 11:
                        norm_scale(norms(0, k), 4 * g)
                    if kind == "LN" and s == 12:
                        stat_low(product, step, g, act_out[:])
                    if kind == "LN" and s == 15:
                        pair_low(product, step, g, small_a[g][:], 1)
                    if kind == "MID" and s == 4:
                        stat_low(product, step, g, small_a[g][:])
                    if kind == "MID" and s == 6:
                        dve.wait_ge(pair_used, pair_place(product, step, g) + 1)
                        dve.wait_ge(rest_ready, rest_count(product - 1, GROUPS - 1))
                        nc.vector.tensor_tensor(rest[:, here], small_b[g][:], rest[:, here],
                                                ALU.add).then_inc(rest_ready, 1)
                    if kind in ("ELU", "LAST"):
                        n = elus(product, k)
                        if s == 0:
                            dve.wait_ge(tile_used, used(product, step, TILES - 1))
                            dve.wait_ge(rest_ready, rest_count(product - 1, GROUPS - 1))
                            dve.wait_ge(elu_ready, n - 1)
                            nc.vector.tensor_tensor(pre[:], panel_sums, rest[:, here], ALU.add).then_inc(pre_ready, 1)
                        if s == 2:
                            dve.wait_ge(expo_ready, n - 1)
                            dve.wait_ge(turned, turns(product, k) - 1)
                            dve.wait_ge(pair_lo_ready, pair_place(2, step, g) if product == 2
                                        else pair_place(3, PANELS - 1, 1) + 1)
                            nc.vector.scalar_tensor_tensor(out=act_out[:], in0=expo[:], scalar=1.0, in1=pre[:],
                                                           op0=ALU.subtract, op1=ALU.max).then_inc(elu_ready, 1)
                    if kind == "ELU" and s == 6:
                        stat_low(product, step, g, small_a[g][:])
                    if kind == "ELU" and s == 7:
                        pair_low(product, step, g, act_out[:])
                    if kind == "LAST" and s == 7:
                        dve.wait_ge(turned, turns(product, k))
                        nc.vector.tensor_tensor(xres[:, here], small_a[g][:], xres[:, here],
                                                ALU.add).then_inc(out_ready, 1)

            dve.wait_ge(x_loaded[0], 16)
            norm_stats(0, 0, 0)
            dve.wait_ge(stats_ready, 1)
            norm_meanvar(0)
            norm_scale(1, 0)
            for i in range(TILES):
                k, r = i // 4, i % 4
                if r == 0:
                    stat_low(-1, k // 2, k % 2, act_out[:])
                split_lo(0, True, 0, i)
                if i == 0:
                    dve.wait_ge(w_loaded, 48)
                    raw_w = rest[:, 0:WEIGHTS * P].rearrange("p (w n) -> p w n", n=P)
                    for c in range(2):
                        last = nc.vector.tensor_tensor(raw_w[:, W_ZERO[c], :], raw_w[:, W_ZERO[c], :],
                                                       raw_w[:, W_TWO[c], :], ALU.subtract)
                    last.then_inc(w_sub, 1)
                    dve.wait_ge(w_sub, 1)
                    for c in range(2):
                        last = nc.vector.tensor_scalar(raw_w[:, W_TWO[c], :], raw_w[:, W_TWO[c], :], 2.0, None,
                                                       ALU.mult)
                    last.then_inc(w_made, 1)
                if i == 1:
                    dve.wait_ge(w_hi_ready, 1)
                    nc.vector.tensor_tensor(w_lo[:, :, :], raw_w, w_hi[:, :, :].bitcast(F32),
                                            ALU.subtract).then_inc(w_lo_ready, 1)
                if r == 0 and k + 1 < GROUPS:
                    dve.wait_ge(x_loaded[k + 1], 16)
                    norm_stats((k + 1) // 2, (k + 1) % 2, 4 * k + 4)
                if r == 1:
                    pair_low(-1, k // 2, k % 2, small_a[k % 2][:])
                    if k + 1 < GROUPS:
                        dve.wait_ge(stats_ready, k + 2)
                        norm_meanvar(4 * k + 4)
                if r == 2 and k:
                    if k == 1:
                        dve.wait_ge(w_lo_ready, 1)
                    rest_opening(k - 1)
                if r == 3 and k + 1 < GROUPS:
                    norm_scale(k + 2, 4 * k + 4)
            rest_opening(GROUPS - 1)
            for product in range(5):
                if product:
                    for i in range(TILES):
                        ahead(product - 1, PANELS - 1, i)
                        split_lo(product, True, 0, i)
                        after(product - 1, PANELS - 1, i)
                with dve.Fori(1, PANELS) as step:
                    for i in range(TILES):
                        ahead(product, step - 1, i)
                        split_lo(product, False, step, i)
                        after(product, step - 1, i)
            for i in range(TILES):
                after(4, PANELS - 1, i)

        @block.tensor
        def _(pe):
            def multiply(product, first, step, i):
                buf, t, slot = product % 2, tile_at(product, first, i), slot_at(product, i, SPLIT_SLOTS)
                fresh = not (product and first and i < SPLIT_SLOTS)
                if first:
                    pe.wait_ge(stat_lo_ready, stat(product - 1, i // 4))

                def part(weights, moving, start=False, stop=False):
                    for half in range(2):
                        last = nc.tensor.matmul(sums[:, sum_cols(step, half)], weights[:, blk(t)],
                                                moving[:, slot, half * GROUP:(half + 1) * GROUP],
                                                start=start, stop=stop)
                    return last

                if fresh:
                    pe.wait_ge(hi_ready, splits(product, step, i))
                part(s_lo[buf], a_hi, start=(i == 0))
                part(s_hi[buf], a_hi)
                if fresh:
                    pe.wait_ge(lo_ready, splits(product, step, i))
                part(s_hi[buf], a_lo, stop=(i == TILES - 1)).then_inc(tile_used, 1)

            def pair_rows(dst, w):
                for b in range(4):
                    nc.tensor.matmul(dst[:, blk(b)], pair_hi[:, blk(b)], w_hi[:, w, :], start=True, stop=False)
                    nc.tensor.matmul(dst[:, blk(b)], pair_hi[:, blk(b)], w_lo[:, w, :], start=False, stop=False)
                    last = nc.tensor.matmul(dst[:, blk(b)], pair_lo[:, blk(b)], w_hi[:, w, :], start=False, stop=True)
                return last

            def pair_columns(dst, w):
                nc.tensor.matmul(dst[:], w_lo[:, w, :], pair_hi[:], start=True, stop=False)
                nc.tensor.matmul(dst[:], w_hi[:, w, :], pair_hi[:], start=False, stop=False)
                return nc.tensor.matmul(dst[:], w_hi[:, w, :], pair_lo[:], start=False, stop=True)

            def turn(dst):
                for b in range(4):
                    last = nc.tensor.transpose(dst[:, blk(b)], act_out[:, blk(b)], ident[:])
                last.then_inc(turned, 1)

            def after(product, step, i):
                kind = AFTER[product]
                for g in range(2):
                    k = 2 * step + g
                    s = i - LAG - STAGGER * g
                    if kind == "LN" and s == 0:
                        pe.wait_ge(pair_lo_ready, pair_place(product, step, g) + 1)
                        pair_rows(small_a[g], W_NEIGH).then_inc(pair_used, 1)
                    if kind == "LN" and s == 11:
                        pe.wait_ge(norm_ready, norms(product, k))
                        pe.wait_ge(pre_ready, k + 1)
                        turn(small_a[g])
                    if kind == "LN" and s == 15:
                        pe.wait_ge(pair_lo_ready, pair_place(product, step, g, 1) + 1)
                        pe.wait_ge(rest_ready, rest_count(product, k) - 2)
                        pair_columns(small_b[g], W_ZERO[0]).then_inc(pair_used, 1)
                    if kind == "MID" and s == 0:
                        pe.wait_ge(pair_lo_ready, pair_place(product, step, g) + 1)
                        pe.wait_ge(stat_lo_ready, stat(product, k) - 2)
                        pe.wait_ge(rest_ready, rest_count(product, k) - 2)
                        pair_rows(small_a[g], W_TWO[conv(product)])
                        pair_columns(small_b[g], W_ONE[conv(product)]).then_inc(pair_used, 1)
                    if kind in ("ELU", "LAST") and s == 3:
                        pe.wait_ge(elu_ready, elus(product, k))
                        if product == 2:
                            pe.wait_ge(stat_lo_ready, stat(product, k) - 2)
                        turn(small_a[g])
                    if kind == "ELU" and s == 7:
                        pe.wait_ge(pair_lo_ready, pair_place(product, step, g) + 1)
                        pe.wait_ge(rest_ready, rest_count(product, k) - 2)
                        pair_columns(small_b[g], W_ZERO[1]).then_inc(pair_used, 1)

            pe.wait_ge(ident_ready, 1)
            for i in range(TILES):
                k, r = i // 4, i % 4
                if r == 0:
                    pe.wait_ge(norm_ready, k + 1)
                    if k >= 2:
                        pe.wait_ge(pair_lo_ready, k - 1)
                    turn(small_a[k % 2])
                multiply(0, True, 0, i)
                if r == 2:
                    if k == 0:
                        pe.wait_ge(w_lo_ready, 1)
                    pe.wait_ge(pair_lo_ready, k + 1)
                    if k >= 2:
                        pe.wait_ge(rest_ready, k - 1)
                    pair_rows(small_b[k % 2], W_SELF).then_inc(pair_used, 1)
            for product in range(5):
                if product:
                    for i in range(TILES):
                        multiply(product, True, 0, i)
                        after(product - 1, PANELS - 1, i)
                with pe.Fori(1, PANELS) as step:
                    for i in range(TILES):
                        multiply(product, False, step, i)
                        after(product, step - 1, i)
            for i in range(TILES):
                after(4, PANELS - 1, i)


def kernel(**inputs):
    import numpy as np
    import concourse.bacc as bacc
    from concourse import mybir as mb
    from concourse.bass_utils import run_bass_kernel_spmd

    a = {k: np.asarray(v) for k, v in inputs.items()}

    def rows(m):
        return np.ascontiguousarray(m.reshape(-1, P, P).transpose(1, 0, 2).reshape(P, -1))

    tiles = a["adj"].reshape(PANELS, PANEL, TILES, P).transpose(0, 2, 3, 1)
    arrays = {
        "x": rows(a["x"]),
        "adj_tiles": np.ascontiguousarray(tiles).reshape(PANELS * TILES, P, PANEL),
        "w0t": rows(a["L0_gnn_W"].T),
        "w1": rows(a["L1_gnn_W0"].reshape(-1, P)),
        "w2": rows(a["L1_gnn_W1"].reshape(-1, P)),
        "b0": np.ascontiguousarray(np.broadcast_to(a["L0_gnn_b"], (P, P))),
        "b1": a["L1_gnn_b0"].reshape(P, 1),
        "b2": a["L1_gnn_b1"].reshape(P, 1),
    }
    nc = bacc.Bacc("TRN2", target_bir_lowering=False, num_devices=1)
    args = [nc.dram_tensor(f"in_{k}", v.shape, mb.dt.from_np(v.dtype), kind="ExternalInput").ap()
            for k, v in arrays.items()]
    out = nc.dram_tensor("out", (P, N), F32, kind="ExternalOutput").ap()
    build(nc, *args, out)
    r = run_bass_kernel_spmd(nc, [{f"in_{k}": v for k, v in arrays.items()}], core_ids=[0])
    got = r.results[0]["out"]
    return np.ascontiguousarray(got.reshape(P, BLOCKS, P).transpose(1, 0, 2)).reshape(N, P)
```

```python
from contextlib import ExitStack

import concourse.bass as bass
from concourse import mybir

F32 = mybir.dt.float32
F32R = mybir.dt.float32r
ALU = mybir.AluOpType
ACT = mybir.ActivationFunctionType

P = 128
N = 4096
BLOCKS = N // P
PANEL = 1024
PANELS = N // PANEL
TILES = BLOCKS
KEPT = 15
KEPT_TILES = 2
LOADED = TILES - KEPT_TILES
GROUP = 512
GROUPS = N // GROUP
PAIRS = LOADED // 2
RAW_SLOTS = 5
SPLIT_SLOTS = 4
EPS = 1e-5
DIRECT_UNTIL = 16
DIRECT_OF_4 = 1
DIRECT = (4, 13, 22)
LAG = 2
STAGGER = {"LN": 10, "MID": 12, "ELU": 12, "LAST": 12}

AFTER = ["LN", "MID", "ELU", "MID", "LAST"]
W_SELF, W_NEIGH = 0, 1
W_ZERO = {0: 2, 1: 5}
W_ONE = {0: 3, 1: 6}
W_TWO = {0: 4, 1: 7}
WEIGHTS = 8
WARM_UP = 20




def forward(product, first):
    return first if product == 0 else product % 2 == 1


def tile_at(product, first, i):
    return i if forward(product, first) else TILES - 1 - i


def panel_at(product, step):
    return step if product % 2 == 0 else (3 * step + 3) & 3


def half_at(product, g):
    return g if product % 2 == 0 else 1 - g


def slot_at(product, n, slots):
    return n % slots if product % 2 == 0 else slots - 1 - n % slots


def direct(product, first, i):
    return product == 0 and (i < DIRECT_UNTIL and i % 4 < DIRECT_OF_4 if first else i in DIRECT)


def loaded_number(i):
    return i if i < KEPT else i - KEPT_TILES


def place_of(q):
    return q if q < KEPT else q + KEPT_TILES


def multiplications(product, panel, g, again=0):
    if product < 0:
        return 2 * panel + g
    if product == 0:
        return GROUPS + 4 * panel + 2 * again + g
    return 3 * GROUPS + GROUPS * (product - 1) + 2 * panel + g


def build(nc, x, adj_pairs, adj_kept, weights, b0, b12, out):
    with ExitStack() as ctx:
        def sb(name, shape, dt=F32):
            return ctx.enter_context(nc.sbuf_tensor(name, shape, dt))

        def sem(name):
            return ctx.enter_context(nc.semaphore(name))

        s_hi = [sb(f"s_hi{i}", [P, N], F32R) for i in range(2)]
        s_lo = [sb(f"s_lo{i}", [P, N], F32R) for i in range(2)]
        rest = sb("rest", [P, N])
        xres = sb("xres", [P, N])
        raw = sb("raw", [P, RAW_SLOTS, 2 * PANEL])
        kept = sb("kept", [P, PANELS * KEPT_TILES * PANEL])
        a_hi = sb("a_hi", [P, SPLIT_SLOTS, PANEL], F32R)
        a_lo = sb("a_lo", [P, SPLIT_SLOTS, PANEL], F32R)
        w = sb("w", [P, WEIGHTS, P])
        operand = sb("operand", [P, GROUP])
        pre = sb("pre", [P, GROUP])
        expo = sb("expo", [P, GROUP])
        act_out = sb("act_out", [P, GROUP])
        late_pre = [pre, sb("pre2", [P, GROUP])]
        late_expo = [expo, sb("expo2", [P, GROUP])]
        late_out = [act_out, sb("act_out2", [P, GROUP])]
        opening = [act_out, pre]
        ident = sb("ident", [P, P])
        bias0 = sb("bias0", [P, P])
        bias_col = sb("bias_col", [P, 2])
        plain = sb("plain", [P, len(DIRECT) * P])
        eps = sb("eps", [P, 1])
        warm = sb("warm", [P, 1])
        stats = sb("stats", [P, BLOCKS, 6])
        meanvar = sb("meanvar", [P, BLOCKS, 2])
        std = sb("std", [P, BLOCKS])
        rstd = sb("rstd", [P, BLOCKS])
        shift = sb("shift", [P, BLOCKS])

        sums = ctx.enter_context(nc.psum_tensor("sums", [P, 2 * PANEL], F32))
        small_a = [ctx.enter_context(nc.psum_tensor(f"small_a{i}", [P, GROUP], F32)) for i in range(2)]
        small_b = [ctx.enter_context(nc.psum_tensor(f"small_b{i}", [P, GROUP], F32)) for i in range(2)]

        x_loaded = [sem(f"x_loaded{i}") for i in range(GROUPS)]
        w_loaded = sem("w_loaded")
        bias_loaded = sem("bias_loaded")
        raw_loaded = [sem(f"raw_loaded{i}") for i in range(RAW_SLOTS)]
        kept_loaded = sem("kept_loaded")
        zeros_ready = sem("zeros_ready")
        ident_ready = sem("ident_ready")
        eps_ready = sem("eps_ready")
        w_sub = sem("w_sub")
        w_made = sem("w_made")
        hi_ready = sem("hi_ready")
        lo_ready = sem("lo_ready")
        tile_used = sem("tile_used")
        operand_ready = sem("operand_ready")
        multiplied = sem("multiplied")
        stat_hi_ready = sem("stat_hi_ready")
        stat_lo_ready = sem("stat_lo_ready")
        rest_ready = sem("rest_ready")
        plain_ready = sem("plain_ready")
        pre_ready = sem("pre_ready")
        res_ready = sem("res_ready")
        stats_ready = sem("stats_ready")
        meanvar_ready = sem("meanvar_ready")
        std_ready = sem("std_ready")
        rstd_ready = sem("rstd_ready")
        shift_ready = sem("shift_ready")
        neg_ready = sem("neg_ready")
        expo_ready = sem("expo_ready")
        norm_ready = sem("norm_ready")
        elu_ready = sem("elu_ready")
        turned = sem("turned")
        out_ready = sem("out_ready")
        stored = sem("stored")

        def used(product, step, i):
            return (product * PANELS + step) * TILES + i + 1

        def splits(product, step, i):
            if product == 0 and isinstance(step, int) and step == 0:
                return sum(not direct(0, True, n) for n in range(i + 1))
            if product:
                return (used(product, step, i) - SPLIT_SLOTS * product - DIRECT_UNTIL // 4 * DIRECT_OF_4
                        - (PANELS - 1) * len(DIRECT))
            return (TILES - len(DIRECT)) * step + (i + 1 - sum(n <= i for n in DIRECT)
                                                   - DIRECT_UNTIL // 4 * DIRECT_OF_4 + len(DIRECT))

        def splits_before(product):
            return splits(product - 1, PANELS - 1, TILES - 1)

        def loads(product, step, q):
            return (PAIRS // RAW_SLOTS * PANELS - 1) * product + PAIRS // RAW_SLOTS * step + q // RAW_SLOTS + 1

        def stat(product, k):
            return (product + 1) * GROUPS + k + 1

        rest_count = stat

        def norms(product, k):
            return (product + 1) * GROUPS + k + 1

        def elus(product, k):
            return 1 + (GROUPS if product == 4 else 0) + k + 1

        def residuals(k):
            return 1 + k + 1

        def turns(product, k):
            return {-1: 0, 0: 1, 2: 2, 4: 3}[product] * GROUPS + k + 1

        def elu_buffers(product, g):
            if product == 4:
                return late_pre[g], late_expo[g], late_out[g], 1 + g
            return pre, expo, act_out, 1

        def operands(product, step, g, again=0):
            return multiplications(product, step, g, again) + 1 - (GROUPS if product == 3 else 0)

        def cols(product, step, g):
            return bass.ds(panel_at(product, step) * PANEL + half_at(product, g) * GROUP, GROUP)

        def sum_cols(step, half):
            return bass.ds((step % 2) * PANEL + half * GROUP, GROUP)

        def blk(b):
            return slice(b * P, (b + 1) * P)

        def source(product, first, step, i):
            t = tile_at(product, first, i)
            if KEPT <= t < KEPT + KEPT_TILES:
                return kept[:, bass.ds((panel_at(product, step) * KEPT_TILES + t - KEPT) * PANEL, PANEL)]
            half = loaded_number(t) % 2
            return raw[:, slot_at(product, loaded_number(i) // 2, RAW_SLOTS), half * PANEL:(half + 1) * PANEL]

        def conv(product):
            return 0 if product < 3 else 1

        block = ctx.enter_context(nc.Block())

        @block.sync
        def _(sp):
            def load(product, first, step, q):
                if q >= RAW_SLOTS:
                    before = [place_of(2 * (q - RAW_SLOTS) + n) for n in range(2)]
                    if any(direct(product, first, i) for i in before):
                        sp.wait_ge(tile_used, used(product, step, before[1]))
                    elif product and first and before[1] < SPLIT_SLOTS:
                        sp.wait_ge(lo_ready, splits_before(product))
                    else:
                        sp.wait_ge(lo_ready, splits(product, step, before[1]))
                elif not first:
                    before = place_of(2 * (q + PAIRS - RAW_SLOTS) + 1)
                    if product == 0:
                        sp.wait_ge(tile_used, used(product, step - 1, before))
                    else:
                        sp.wait_ge(lo_ready, splits(product, step - 1, before))
                pair = q if forward(product, first) else PAIRS - 1 - q
                slot = slot_at(product, q, RAW_SLOTS)
                sp.dma_start(raw[:, slot, :], adj_pairs[bass.ds(panel_at(product, step) * PAIRS + pair, 1), :, :]
                             ).then_inc(raw_loaded[slot], 16)

            def load_kept(first, step):
                if not first:
                    sp.wait_ge(kept_loaded, 16 * step)
                sp.dma_start(kept[:, bass.ds(step * KEPT_TILES * PANEL, KEPT_TILES * PANEL)],
                             adj_kept[bass.ds(step, 1), :, :]).then_inc(kept_loaded, 16)

            def load_x(k):
                sp.dma_start(xres[:, k * GROUP:(k + 1) * GROUP],
                             x[:, k * GROUP:(k + 1) * GROUP]).then_inc(x_loaded[k], 16)

            def store(step):
                for g in range(2):
                    sp.wait_ge(out_ready, 2 * step + g + 1)
                    where = bass.ds(step * PANEL + g * GROUP, GROUP)
                    sp.dma_start(out[:, where], xres[:, where]).then_inc(stored, 16)

            def panel_loads(product, first, step):
                for q in range(RAW_SLOTS if product and first else 0, PAIRS):
                    load(product, first, step, q)
                    if product == 0 and first and q == 0:
                        load_x(1)
                    if product == 0 and first and q % 2 == 0 and q // 2 + 2 < GROUPS:
                        load_x(q // 2 + 2)
                    if product == 0 and first and q == 3:
                        sp.dma_start(bias0[:], b0).then_inc(bias_loaded, 16)
                        sp.dma_start(bias_col[:], b12).then_inc(bias_loaded, 16)
                    if product == 0 and q == KEPT // 2 - RAW_SLOTS:
                        load_kept(first, step)
                    if product == 4 and not first and q == PAIRS - 2:
                        store(step - 1)

            load_x(0)
            for product in range(5):
                panel_loads(product, True, 0)
                with sp.Fori(1, PANELS) as step:
                    panel_loads(product, False, step)
            store(PANELS - 1)
            sp.wait_ge(stored, 16 * GROUPS)

        @block.gpsimd
        def _(pool):
            nc.gpsimd.memset(eps[:], EPS).then_inc(eps_ready, 1)
            nc.gpsimd.memset(expo[:], 0.0).then_inc(elu_ready, 1)
            nc.gpsimd.memset(pre[:], 0.0).then_inc(res_ready, 1)
            nc.gpsimd.memset(ident[:], 0.0).then_inc(zeros_ready, 1)
            pool.wait_ge(zeros_ready, 1)
            nc.gpsimd.affine_select(out=ident[:], in_=ident[:], compare_op=ALU.not_equal, fill=1.0,
                                    base=0, pattern=[[-1, P]], channel_multiplier=1
                                    ).then_inc(ident_ready, 1)

            def stat_low(product, step, g, src):
                pool.wait_ge(stat_hi_ready, stat(product, 2 * step + g))
                buf, where = (product + 1) % 2, cols(0, step, g)
                nc.gpsimd.tensor_tensor(s_lo[buf][:, where], src, s_hi[buf][:, where].bitcast(F32),
                                        ALU.subtract).then_inc(stat_lo_ready, 1)

            for k in range(GROUPS):
                stat_low(-1, k // 2, k % 2, opening[k % 2][:])
            with pool.Fori(0, PANELS) as step:
                for g in range(2):
                    stat_low(0, step, g, act_out[:])

        @block.scalar
        def _(act):
            def split_hi(product, first, step, i):
                if (product and first and i < SPLIT_SLOTS) or direct(product, first, i):
                    return
                t = tile_at(product, first, i)
                if KEPT <= t < KEPT + KEPT_TILES:
                    if product == 0:
                        act.wait_ge(kept_loaded, 16 * (step + 1))
                else:
                    q = loaded_number(i) // 2
                    if not (product and first and q < RAW_SLOTS):
                        act.wait_ge(raw_loaded[slot_at(product, q, RAW_SLOTS)], 16 * loads(product, step, q))
                if not (product == 0 and first and i < SPLIT_SLOTS):
                    act.wait_ge(tile_used, used(product, step, i - SPLIT_SLOTS))
                nc.scalar.activation(a_hi[:, slot_at(product, i, SPLIT_SLOTS), :], source(product, first, step, i),
                                     ACT.Copy).then_inc(hi_ready, 1)

            def sums_to_operand(product, step, g):
                act.wait_ge(tile_used, used(product, step, TILES - 1))
                act.wait_ge(multiplied, multiplications(product, step, g))
                nc.scalar.activation(operand[:], sums[:, sum_cols(step, half_at(product, g))],
                                     ACT.Copy).then_inc(operand_ready, 1)

            def norm_std(n, first):
                act.wait_ge(meanvar_ready, n)
                nc.scalar.activation(std[:, first:first + 4], meanvar[:, first:first + 4, 1], ACT.Sqrt,
                                     bias=eps[:]).then_inc(std_ready, 1)

            def norm_opening(k):
                act.wait_ge(shift_ready, k + 1)
                if k == 1:
                    act.wait_ge(res_ready, 1)
                if k >= 2:
                    act.wait_ge(turned, k - 1)
                    act.wait_ge(stat_lo_ready, k - 1)
                    act.wait_ge(tile_used, used(0, 0, 4 * (k - 2) + DIRECT_OF_4 - 1))
                for b in range(4):
                    last = nc.scalar.activation(opening[k % 2][:, blk(b)], xres[:, (4 * k + b) * P:(4 * k + b + 1) * P],
                                                ACT.Relu, bias=shift[:, 4 * k + b:4 * k + b + 1],
                                                scale=rstd[:, 4 * k + b:4 * k + b + 1])
                last.then_inc(norm_ready, 1)

            def stat_opening(k):
                act.wait_ge(norm_ready, k + 1)
                nc.scalar.activation(s_hi[0][:, k * GROUP:(k + 1) * GROUP], opening[k % 2][:],
                                     ACT.Copy).then_inc(stat_hi_ready, 1)
                for n, i in enumerate(DIRECT):
                    t = tile_at(0, False, i)
                    if t // 4 == k:
                        nc.scalar.activation(plain[:, blk(n)], opening[k % 2][:, blk(t % 4)],
                                             ACT.Copy).then_inc(plain_ready, 1)

            def norm_apply(product, step, g, first):
                k = 2 * step + g
                act.wait_ge(shift_ready, norms(product, k))
                act.wait_ge(turned, norms(product, k - 1))
                act.wait_ge(stat_lo_ready, stat(product, k - 1))
                for b in range(4):
                    last = nc.scalar.activation(act_out[:, blk(b)],
                                                xres[:, bass.ds(step * PANEL + (4 * g + b) * P, P)], ACT.Relu,
                                                bias=shift[:, first + b:first + b + 1],
                                                scale=rstd[:, first + b:first + b + 1])
                last.then_inc(norm_ready, 1)
                act.wait_ge(norm_ready, norms(product, k))
                nc.scalar.activation(s_hi[(product + 1) % 2][:, cols(0, step, g)], act_out[:],
                                     ACT.Copy).then_inc(stat_hi_ready, 1)

            def turned_to_operand(product, step, g):
                act.wait_ge(turned, turns(product, 2 * step + g))
                act.wait_ge(multiplied, multiplications(product, step, g, 1))
                nc.scalar.activation(operand[:], small_a[g][:], ACT.Copy).then_inc(operand_ready, 1)

            def stat_high(product, step, g):
                nc.scalar.activation(s_hi[(product + 1) % 2][:, cols(product, step, g)], small_a[g][:],
                                     ACT.Copy).then_inc(stat_hi_ready, 1)

            def rest_from_product(product, step, g):
                act.wait_ge(multiplied, multiplications(product, step, g, 1) + 1)
                if product == 0:
                    act.wait_ge(bias_loaded, 32)
                c = 0 if product == 0 else 1
                nc.scalar.activation(rest[:, cols(product, step, g)], small_b[g][:], ACT.Identity,
                                     bias=bias_col[:, c:c + 1]).then_inc(rest_ready, 1)

            def after(product, step, i, tail=False):
                kind = AFTER[product]
                for g in range(2):
                    k = 2 * step + g
                    s = i - LAG - (1 if tail else STAGGER[AFTER[product]]) * g
                    if kind in ("LN", "MID") and s == 0:
                        sums_to_operand(product, step, g)
                    if kind == "LN" and s == 9:
                        norm_std(norms(0, k), 4 * g)
                    if kind == "LN" and s == 12:
                        norm_apply(product, step, g, 4 * g)
                    if kind == "LN" and s == 15:
                        turned_to_operand(product, step, g)
                    if kind == "LN" and s == 19:
                        rest_from_product(product, step, g)
                    if kind == "MID" and s == 4:
                        act.wait_ge(multiplied, multiplications(product, step, g) + 1)
                        stat_high(product, step, g)
                    if kind in ("ELU", "LAST") and s == 1:
                        n = elus(product, k)
                        v, e, _, before = elu_buffers(product, g)
                        act.wait_ge(pre_ready, GROUPS + n - 1)
                        act.wait_ge(elu_ready, n - before)
                        nc.scalar.activation(e[:], v[:], ACT.Relu, scale=-1.0).then_inc(neg_ready, 1)
                        act.wait_ge(neg_ready, n - 1)
                        nc.scalar.activation(e[:], e[:], ACT.Exp, scale=-1.0).then_inc(expo_ready, 1)
                    if kind == "ELU" and s == 7:
                        act.wait_ge(turned, turns(product, k))
                        stat_high(product, step, g)
                    if kind == "ELU" and s == 13:
                        rest_from_product(product, step, g)

            act.wait_ge(eps_ready, 1)
            nc.scalar.activation(warm[:], eps[:], ACT.Sqrt)
            act.dma_start(w[:].rearrange("p w n -> p (w n)"), weights).then_inc(w_loaded, 16)
            norm_std(1, 0)
            norm_opening(0)
            stat_opening(0)
            norm_std(2, 4)
            for i in range(TILES):
                k, r = i // 4, i % 4
                split_hi(0, True, 0, i)
                if r == 1 and k + 1 < GROUPS:
                    norm_opening(k + 1)
                if r == 2 and k + 1 < GROUPS:
                    stat_opening(k + 1)
                if r == 3 and k + 2 < GROUPS:
                    norm_std(k + 3, 4 * k + 8)
                if r == 3:
                    turned_to_operand(-1, k // 2, k % 2)
            for product in range(5):
                if product:
                    for i in range(TILES):
                        split_hi(product, True, 0, i)
                        after(product - 1, PANELS - 1, i)
                with act.Fori(1, PANELS) as step:
                    for i in range(TILES):
                        split_hi(product, False, step, i)
                        after(product, step - 1, i)
            for i in range(TILES):
                after(4, PANELS - 1, i, tail=True)

        @block.vector
        def _(dve):
            def split_lo(product, first, step, i):
                if (product and first and i < SPLIT_SLOTS) or direct(product, first, i):
                    return
                dve.wait_ge(hi_ready, splits(product, step, i))
                slot = slot_at(product, i, SPLIT_SLOTS)
                nc.vector.tensor_tensor(a_lo[:, slot, :], source(product, first, step, i),
                                        a_hi[:, slot, :].bitcast(F32), ALU.subtract).then_inc(lo_ready, 1)

            def stat_low(product, step, g, src):
                dve.wait_ge(stat_hi_ready, stat(product, 2 * step + g))
                buf, where = (product + 1) % 2, cols(max(product, 0), step, g)
                nc.vector.tensor_tensor(s_lo[buf][:, where], src, s_hi[buf][:, where].bitcast(F32),
                                        ALU.subtract).then_inc(stat_lo_ready, 1)

            def norm_stats(step, g, first):
                for b in range(4):
                    last = nc.vector.bn_stats(stats[:, first + b, :],
                                              xres[:, bass.ds(step * PANEL + (4 * g + b) * P, P)])
                last.then_inc(stats_ready, 1)

            def norm_meanvar(first):
                for b in range(4):
                    last = nc.vector.bn_aggr(meanvar[:, first + b, :], stats[:, first + b, :])
                last.then_inc(meanvar_ready, 1)

            def norm_scale(n, first):
                where = slice(first, first + 4)
                dve.wait_ge(std_ready, n)
                nc.vector.reciprocal(rstd[:, where], std[:, where]).then_inc(rstd_ready, 1)
                dve.wait_ge(rstd_ready, n)
                nc.vector.scalar_tensor_tensor(out=shift[:, where], in0=meanvar[:, where, 0], scalar=-1.0,
                                               in1=rstd[:, where], op0=ALU.mult, op1=ALU.mult
                                               ).then_inc(shift_ready, 1)

            def rest_opening(k):
                dve.wait_ge(multiplied, k + 1)
                if k == 0:
                    dve.wait_ge(bias_loaded, 32)
                for b in range(4):
                    last = nc.vector.tensor_tensor(rest[:, k * GROUP + b * P:k * GROUP + (b + 1) * P],
                                                   small_b[k % 2][:, blk(b)], bias0[:], ALU.add)
                last.then_inc(rest_ready, 1)

            def ahead(product, step, i):
                for g in range(2):
                    k = 2 * step + g
                    s = i - LAG - STAGGER[AFTER[product]] * g
                    if AFTER[product] == "LN" and s == 6:
                        dve.wait_ge(res_ready, residuals(k))
                    if AFTER[product] == "LN" and s == 8:
                        dve.wait_ge(stats_ready, norms(0, k))

            def after(product, step, i, tail=False):
                kind = AFTER[product]
                for g in range(2):
                    k = 2 * step + g
                    s = i - LAG - (1 if tail else STAGGER[AFTER[product]]) * g
                    here = cols(product, step, g)
                    panel_sums = sums[:, sum_cols(step, half_at(product, g))]
                    if kind == "LN" and s == 4:
                        dve.wait_ge(multiplied, multiplications(product, step, g) + 1)
                        dve.wait_ge(rest_ready, GROUPS)
                        dve.wait_ge(res_ready, residuals(k) - 1)
                        nc.vector.tensor_tensor(pre[:], small_a[g][:], rest[:, here], ALU.add).then_inc(pre_ready, 1)
                    if kind == "LN" and s == 5:
                        dve.wait_ge(pre_ready, k + 1)
                        nc.vector.scalar_tensor_tensor(out=xres[:, here], in0=pre[:], scalar=0.0,
                                                       in1=xres[:, here], op0=ALU.max,
                                                       op1=ALU.add).then_inc(res_ready, 1)
                    if kind == "LN" and s == 6:
                        norm_stats(step, g, 4 * g)
                    if kind == "LN" and s == 8:
                        norm_meanvar(4 * g)
                    if kind == "LN" and s == 10:
                        norm_scale(norms(0, k), 4 * g)
                    if kind == "MID" and s == 4:
                        stat_low(product, step, g, small_a[g][:])
                    if kind == "MID" and s == 8:
                        dve.wait_ge(multiplied, multiplications(product, step, g) + 1)
                        dve.wait_ge(rest_ready, rest_count(product - 1, GROUPS - 1))
                        nc.vector.tensor_tensor(rest[:, here], small_b[g][:], rest[:, here],
                                                ALU.add).then_inc(rest_ready, 1)
                    if kind in ("ELU", "LAST"):
                        n = elus(product, k)
                        v, e, y, before = elu_buffers(product, g)
                        if s == 0:
                            dve.wait_ge(tile_used, used(product, step, TILES - 1))
                            dve.wait_ge(rest_ready, rest_count(product - 1, GROUPS - 1))
                            dve.wait_ge(elu_ready, n - before)
                            nc.vector.tensor_tensor(v[:], panel_sums, rest[:, here], ALU.add).then_inc(pre_ready, 1)
                        if s == 2:
                            dve.wait_ge(expo_ready, n - 1)
                            dve.wait_ge(turned, turns(product, k) - before)
                            dve.wait_ge(multiplied, multiplications(2, step, g) if product == 2
                                        else multiplications(3, 0, 0))
                            nc.vector.scalar_tensor_tensor(out=y[:], in0=e[:], scalar=1.0, in1=v[:],
                                                           op0=ALU.subtract, op1=ALU.max).then_inc(elu_ready, 1)
                    if kind == "ELU" and s == 6:
                        stat_low(product, step, g, small_a[g][:])
                    if kind == "LAST" and s == 7:
                        dve.wait_ge(turned, turns(product, k))
                        nc.vector.tensor_tensor(xres[:, here], small_a[g][:], xres[:, here],
                                                ALU.add).then_inc(out_ready, 1)

            for k in range(2):
                dve.wait_ge(x_loaded[k], 16)
                norm_stats(0, k, 4 * k)
                dve.wait_ge(stats_ready, k + 1)
                norm_meanvar(4 * k)
                norm_scale(k + 1, 4 * k)
            for i in range(TILES):
                k, r = i // 4, i % 4
                split_lo(0, True, 0, i)
                if i == 0:
                    dve.wait_ge(w_loaded, 16)
                    for c in range(2):
                        last = nc.vector.tensor_tensor(w[:, W_ZERO[c], :], w[:, W_ZERO[c], :], w[:, W_TWO[c], :],
                                                       ALU.subtract)
                    last.then_inc(w_sub, 1)
                    dve.wait_ge(w_sub, 1)
                    for c in range(2):
                        last = nc.vector.tensor_scalar(w[:, W_TWO[c], :], w[:, W_TWO[c], :], 2.0, None, ALU.mult)
                    last.then_inc(w_made, 1)
                if r == 0 and k + 2 < GROUPS:
                    dve.wait_ge(x_loaded[k + 2], 16)
                    norm_stats((k + 2) // 2, k % 2, 4 * k + 8)
                if r == 1:
                    if k + 2 < GROUPS:
                        dve.wait_ge(stats_ready, k + 3)
                        norm_meanvar(4 * k + 8)
                if r == 3:
                    if k:
                        rest_opening(k - 1)
                    if k + 2 < GROUPS:
                        norm_scale(k + 3, 4 * k + 8)
            rest_opening(GROUPS - 1)
            for product in range(5):
                if product:
                    for i in range(TILES):
                        ahead(product - 1, PANELS - 1, i)
                        split_lo(product, True, 0, i)
                        after(product - 1, PANELS - 1, i)
                with dve.Fori(1, PANELS) as step:
                    for i in range(TILES):
                        ahead(product, step - 1, i)
                        split_lo(product, False, step, i)
                        after(product, step - 1, i)
            for i in range(TILES):
                after(4, PANELS - 1, i, tail=True)

        @block.tensor
        def _(pe):
            def multiply(product, first, step, i):
                buf, t, slot = product % 2, tile_at(product, first, i), slot_at(product, i, SPLIT_SLOTS)
                fresh = not (product and first and i < SPLIT_SLOTS)
                if first:
                    pe.wait_ge(stat_lo_ready, stat(product - 1, i // 4))

                def part(weights, moving, start=False, stop=False):
                    for half in range(2):
                        last = nc.tensor.matmul(sums[:, sum_cols(step, half)], weights[:, blk(t)],
                                                moving[:, slot, half * GROUP:(half + 1) * GROUP],
                                                start=start, stop=stop)
                    return last

                if fresh:
                    pe.wait_ge(hi_ready, splits(product, step, i))
                part(s_lo[buf], a_hi, start=(i == 0))
                part(s_hi[buf], a_hi)
                if fresh:
                    pe.wait_ge(lo_ready, splits(product, step, i))
                part(s_hi[buf], a_lo, stop=(i == TILES - 1)).then_inc(tile_used, 1)

            def rows_of(dst, which):
                for b in range(4):
                    last = nc.tensor.matmul(dst[:, blk(b)], operand[:, blk(b)], w[:, which, :], start=True, stop=True)
                return last

            def columns_of(dst, which, src=operand):
                return nc.tensor.matmul(dst[:], w[:, which, :], src[:], start=True, stop=True)

            def multiply_direct(first, step, i):
                t = tile_at(0, first, i)
                if KEPT <= t < KEPT + KEPT_TILES:
                    pe.wait_ge(kept_loaded, 16 * (step + 1))
                else:
                    q = loaded_number(i) // 2
                    pe.wait_ge(raw_loaded[q % RAW_SLOTS], 16 * loads(0, step, q))
                if first:
                    pe.wait_ge(norm_ready, i // 4 + 1)
                    weights = opening[i // 4 % 2][:, blk(i % 4)]
                else:
                    pe.wait_ge(plain_ready, len(DIRECT))
                    weights = plain[:, blk(DIRECT.index(i))]
                tile = source(0, first, step, i)
                for half in range(2):
                    last = nc.tensor.matmul(sums[:, sum_cols(step, half)], weights,
                                            tile[:, half * GROUP:(half + 1) * GROUP], start=(i == 0), stop=False)
                last.then_inc(tile_used, 1)

            def turn(dst, src=act_out):
                for b in range(4):
                    last = nc.tensor.transpose(dst[:, blk(b)], src[:, blk(b)], ident[:])
                last.then_inc(turned, 1)

            def after(product, step, i, tail=False):
                kind = AFTER[product]
                for g in range(2):
                    k = 2 * step + g
                    s = i - LAG - (1 if tail else STAGGER[AFTER[product]]) * g
                    if kind == "LN" and s == 0:
                        pe.wait_ge(operand_ready, operands(product, step, g))
                        rows_of(small_a[g], W_NEIGH).then_inc(multiplied, 1)
                    if kind == "LN" and s == 12:
                        pe.wait_ge(norm_ready, norms(product, k))
                        pe.wait_ge(pre_ready, k + 1)
                        turn(small_a[g])
                    if kind == "LN" and s == 16:
                        pe.wait_ge(operand_ready, operands(product, step, g, 1))
                        pe.wait_ge(rest_ready, rest_count(product, k) - 2)
                        columns_of(small_b[g], W_ZERO[0]).then_inc(multiplied, 1)
                    if kind == "MID" and s == 0:
                        pe.wait_ge(operand_ready, operands(product, step, g))
                        pe.wait_ge(stat_lo_ready, stat(product, k) - 2)
                        pe.wait_ge(rest_ready, rest_count(product, k) - 2)
                        rows_of(small_a[g], W_TWO[conv(product)])
                        columns_of(small_b[g], W_ONE[conv(product)]).then_inc(multiplied, 1)
                    if kind in ("ELU", "LAST") and s == 2:
                        pe.wait_ge(elu_ready, elus(product, k))
                        if product == 2:
                            pe.wait_ge(stat_lo_ready, stat(product, k) - 2)
                        turn(small_a[g], elu_buffers(product, g)[2])
                    if kind == "ELU" and s == 9:
                        pe.wait_ge(rest_ready, rest_count(product, k) - 2)
                        columns_of(small_b[g], W_ZERO[1], act_out).then_inc(multiplied, 1)

            pe.wait_ge(ident_ready, 1)
            for b in range(WARM_UP):
                nc.tensor.transpose(small_a[1][:, blk(b % 4)], ident[:], ident[:])
            pe.wait_ge(norm_ready, 1)
            turn(small_a[0], opening[0])
            for i in range(TILES):
                k, r = i // 4, i % 4
                if direct(0, True, i):
                    multiply_direct(True, 0, i)
                else:
                    multiply(0, True, 0, i)
                if r == 3:
                    if k == 0:
                        pe.wait_ge(w_made, 1)
                    pe.wait_ge(operand_ready, k + 1)
                    if k >= 2:
                        pe.wait_ge(rest_ready, k - 1)
                    rows_of(small_b[k % 2], W_SELF).then_inc(multiplied, 1)
                if r == 3 and k + 1 < GROUPS:
                    pe.wait_ge(norm_ready, k + 2)
                    if k >= 1:
                        pe.wait_ge(operand_ready, k)
                    turn(small_a[(k + 1) % 2], opening[(k + 1) % 2])
            for product in range(5):
                if product:
                    for i in range(TILES):
                        multiply(product, True, 0, i)
                        after(product - 1, PANELS - 1, i)
                with pe.Fori(1, PANELS) as step:
                    for i in range(TILES):
                        if direct(product, False, i):
                            multiply_direct(False, step, i)
                        else:
                            multiply(product, False, step, i)
                        after(product, step - 1, i)
            for i in range(TILES):
                after(4, PANELS - 1, i, tail=True)


def kernel(**inputs):
    import numpy as np
    import concourse.bacc as bacc
    from concourse import mybir as mb
    from concourse.bass_utils import run_bass_kernel_spmd

    a = {k: np.asarray(v) for k, v in inputs.items()}

    def rows(m):
        return np.ascontiguousarray(m.reshape(-1, P, P).transpose(1, 0, 2).reshape(P, -1))

    tiles = a["adj"].reshape(PANELS, PANEL, TILES, P).transpose(0, 2, 3, 1)

    def pairs(some):
        return np.ascontiguousarray(some.reshape(-1, 2, P, PANEL).transpose(0, 2, 1, 3)).reshape(-1, P, 2 * PANEL)

    arrays = {
        "x": rows(a["x"]),
        "adj_pairs": pairs(np.concatenate([tiles[:, :KEPT], tiles[:, KEPT + KEPT_TILES:]], axis=1)),
        "adj_kept": pairs(tiles[:, KEPT:KEPT + KEPT_TILES]),
        "weights": np.concatenate([rows(a["L0_gnn_W"].T), rows(a["L1_gnn_W0"].reshape(-1, P)),
                                   rows(a["L1_gnn_W1"].reshape(-1, P))], axis=1),
        "b0": np.ascontiguousarray(np.broadcast_to(a["L0_gnn_b"], (P, P))),
        "b12": np.stack([a["L1_gnn_b0"], a["L1_gnn_b1"]], axis=1),
    }
    nc = bacc.Bacc("TRN2", target_bir_lowering=False, num_devices=1,
                   dynamic_dma_scratch_size=1024)
    args = [nc.dram_tensor(f"in_{k}", v.shape, mb.dt.from_np(v.dtype), kind="ExternalInput").ap()
            for k, v in arrays.items()]
    out = nc.dram_tensor("out", (P, N), F32, kind="ExternalOutput").ap()
    build(nc, *args, out)
    r = run_bass_kernel_spmd(nc, [{f"in_{k}": v for k, v in arrays.items()}], core_ids=[0])
    got = r.results[0]["out"]
    return np.ascontiguousarray(got.reshape(P, BLOCKS, P).transpose(1, 0, 2)).reshape(N, P)
```
